# Optimizing a Trainium2 kernel written in Bass

```python
import numpy as np
import jax
import jax.numpy as jnp

def _softmax(x, axis=-1):
    return jax.nn.softmax(x, axis=axis)
def _gelu(x):
    return jax.nn.gelu(x, approximate=True)
def _silu(x):
    return jax.nn.silu(x)
def _sigmoid(x):
    return jax.nn.sigmoid(x)
def _layernorm(x, axis=-1, eps=1e-5):
    m = jnp.mean(x, axis=axis, keepdims=True)
    v = jnp.var(x, axis=axis, keepdims=True)
    return (x - m) / jnp.sqrt(v + eps)
def _scatter_add(tgt, idx, src, axis=0):
    return tgt.at[idx].add(src)
def _segment_sum(src, seg, n):
    return jax.ops.segment_sum(src, seg, n)

kernel_name = 'mk_conv_preact_d2_conv_nchw256_718ce3'

def setup_inputs(seed: int = 0):
    np.random.seed(seed)
    _w = jnp.asarray
    def _rec_inputs():
        import jax
        import jax.numpy as jnp
        _gk = jax.random.key(seed)
        x = -0.0002928 + 1 * jax.random.normal(jax.random.fold_in(_gk, 1), (4, 256, 64, 64), jnp.float32)
        return x
    x = _rec_inputs()
    def _L0_conv_setup():
        import jax, jax.numpy as jnp
        import numpy as np
        K = 3
        PAD = 1
        STRIDE = 1
        DIL = 1

        def _bilinear(img, y, x):
            C, H, W = img.shape
            y0 = jnp.floor(y)
            x0 = jnp.floor(x)
            ly = y - y0
            lx = x - x0
            hy = 1.0 - ly
            hx = 1.0 - lx
            y0i = y0.astype(jnp.int32)
            x0i = x0.astype(jnp.int32)

            def g(iy, ix, w):
                valid = (iy >= 0) & (iy < H) & (ix >= 0) & (ix < W)
                v = img[:, jnp.clip(iy, 0, H - 1), jnp.clip(ix, 0, W - 1)]
                return v * (w * valid)[None]
            return g(y0i, x0i, hy * hx) + g(y0i, x0i + 1, hy * lx) + g(y0i + 1, x0i, ly * hx) + g(y0i + 1, x0i + 1, ly * lx)
        key = jax.random.key(seed)
        k1, k2, k3 = jax.random.split(key, 3)
        B, C, H, W, O = (4, 256, 64, 64, 256)
        x = jax.random.normal(k1, (B, C, H, W), jnp.float32)
        w_off = jax.random.normal(k2, (3 * K * K, C, K, K), jnp.float32) * 0.01
        b_off = jnp.zeros((3 * K * K,), jnp.float32)
        w_conv = jax.random.normal(k3, (O, C, K, K), jnp.float32) * (1.0 / np.sqrt(C * K * K))
        return {'x': x, 'w_off': w_off, 'b_off': b_off, 'w_conv': w_conv}
    _L0_conv_all = _L0_conv_setup()
    _L0_conv_in = {k: v for k, v in _L0_conv_all.items() if k in ('w_off', 'b_off', 'w_conv', )}
    del _L0_conv_all

    def _L1_conv_setup():
        import jax, jax.numpy as jnp
        import numpy as np
        EPS = 1e-05

        def ternary_quantize(w):
            w = w - w.mean()
            mx, mn = (w.max(), w.min())
            third = (mx - mn) / 3
            lo = mn + third
            hi = mx - third
            return jnp.where(w < lo, -1.0, jnp.where(w > hi, 1.0, 0.0)).astype(w.dtype)

        def conv3x3(x, w):
            return jax.lax.conv_general_dilated(x, w, window_strides=(1, 1), padding=((1, 1), (1, 1)), dimension_numbers=('NCHW', 'OIHW', 'NCHW'))

        def batchnorm(x, gamma, beta):
            m = x.mean(axis=(0, 2, 3), keepdims=True)
            v = x.var(axis=(0, 2, 3), keepdims=True)
            xn = (x - m) * jax.lax.rsqrt(v + EPS)
            return xn * gamma.reshape(1, -1, 1, 1) + beta.reshape(1, -1, 1, 1)
        key = jax.random.key(seed)
        ks = jax.random.split(key, 3)
        N, C, H, W = (32, 256, 56, 56)
        x = jax.random.normal(ks[0], (N, C, H, W), dtype=jnp.float32)
        std = 1.0 / np.sqrt(C * 9)
        w1 = jax.random.normal(ks[1], (C, C, 3, 3), dtype=jnp.float32) * std
        w2 = jax.random.normal(ks[2], (C, C, 3, 3), dtype=jnp.float32) * std
        gamma1 = jnp.ones((C,), jnp.float32)
        beta1 = jnp.zeros((C,), jnp.float32)
        gamma2 = jnp.ones((C,), jnp.float32)
        beta2 = jnp.zeros((C,), jnp.float32)
        return {'x': x, 'w1': w1, 'gamma1': gamma1, 'beta1': beta1, 'w2': w2, 'gamma2': gamma2, 'beta2': beta2}
    _L1_conv_all = _L1_conv_setup()
    _L1_conv_in = {k: v for k, v in _L1_conv_all.items() if k in ('w1', 'gamma1', 'beta1', 'w2', 'gamma2', 'beta2', )}
    del _L1_conv_all

    return {
        "x": x,
        "L0_conv_w_off": _L0_conv_in["w_off"],
        "L0_conv_b_off": _L0_conv_in["b_off"],
        "L0_conv_w_conv": _L0_conv_in["w_conv"],
        "L1_conv_w1": _L1_conv_in["w1"],
        "L1_conv_gamma1": _L1_conv_in["gamma1"],
        "L1_conv_beta1": _L1_conv_in["beta1"],
        "L1_conv_w2": _L1_conv_in["w2"],
        "L1_conv_gamma2": _L1_conv_in["gamma2"],
        "L1_conv_beta2": _L1_conv_in["beta2"],
    }

def reference(x, L0_conv_w_off, L0_conv_b_off, L0_conv_w_conv, L1_conv_w1, L1_conv_gamma1, L1_conv_beta1, L1_conv_w2, L1_conv_gamma2, L1_conv_beta2):
    import jax
    import jax.numpy as jnp
    def _L0_conv_ref(x, w_off, b_off, w_conv):
        import jax, jax.numpy as jnp
        import numpy as np
        K = 3
        PAD = 1
        STRIDE = 1
        DIL = 1

        def _bilinear(img, y, x):
            C, H, W = img.shape
            y0 = jnp.floor(y)
            x0 = jnp.floor(x)
            ly = y - y0
            lx = x - x0
            hy = 1.0 - ly
            hx = 1.0 - lx
            y0i = y0.astype(jnp.int32)
            x0i = x0.astype(jnp.int32)

            def g(iy, ix, w):
                valid = (iy >= 0) & (iy < H) & (ix >= 0) & (ix < W)
                v = img[:, jnp.clip(iy, 0, H - 1), jnp.clip(ix, 0, W - 1)]
                return v * (w * valid)[None]
            return g(y0i, x0i, hy * hx) + g(y0i, x0i + 1, hy * lx) + g(y0i + 1, x0i, ly * hx) + g(y0i + 1, x0i + 1, ly * lx)
        B, C, H, W = x.shape
        K2 = K * K
        om = jax.lax.conv_general_dilated(x, w_off, (STRIDE, STRIDE), [(PAD, PAD), (PAD, PAD)], rhs_dilation=(DIL, DIL), dimension_numbers=('NCHW', 'OIHW', 'NCHW')) + b_off[None, :, None, None]
        Ho, Wo = (om.shape[2], om.shape[3])
        off = om[:, :2 * K2].reshape(B, K2, 2, Ho, Wo)
        mask = jax.nn.sigmoid(om[:, 2 * K2:])
        hs = jnp.arange(Ho, dtype=jnp.float32) * STRIDE - PAD
        ws = jnp.arange(Wo, dtype=jnp.float32) * STRIDE - PAD
        ki, kj = jnp.meshgrid(jnp.arange(K, dtype=jnp.float32), jnp.arange(K, dtype=jnp.float32), indexing='ij')
        ki = ki.reshape(K2)
        kj = kj.reshape(K2)
        ys = off[:, :, 0] + hs[None, None, :, None] + (ki * DIL)[None, :, None, None]
        xs = off[:, :, 1] + ws[None, None, None, :] + (kj * DIL)[None, :, None, None]
        sampled = jax.vmap(_bilinear)(x, ys, xs)
        sampled = sampled * mask[:, None]
        O = w_conv.shape[0]
        out = jnp.einsum('bckhw,ock->bohw', sampled, w_conv.reshape(O, C, K2))
        return out

    def _L1_conv_ref(x, w1, gamma1, beta1, w2, gamma2, beta2):
        import jax, jax.numpy as jnp
        import numpy as np
        EPS = 1e-05

        def ternary_quantize(w):
            w = w - w.mean()
            mx, mn = (w.max(), w.min())
            third = (mx - mn) / 3
            lo = mn + third
            hi = mx - third
            return jnp.where(w < lo, -1.0, jnp.where(w > hi, 1.0, 0.0)).astype(w.dtype)

        def conv3x3(x, w):
            return jax.lax.conv_general_dilated(x, w, window_strides=(1, 1), padding=((1, 1), (1, 1)), dimension_numbers=('NCHW', 'OIHW', 'NCHW'))

        def batchnorm(x, gamma, beta):
            m = x.mean(axis=(0, 2, 3), keepdims=True)
            v = x.var(axis=(0, 2, 3), keepdims=True)
            xn = (x - m) * jax.lax.rsqrt(v + EPS)
            return xn * gamma.reshape(1, -1, 1, 1) + beta.reshape(1, -1, 1, 1)
        q1 = ternary_quantize(w1)
        out1 = jax.nn.relu(batchnorm(conv3x3(x, q1), gamma1, beta1))
        q2 = ternary_quantize(w2)
        out2 = batchnorm(conv3x3(out1, q2), gamma2, beta2)
        return jax.nn.relu(out1 + out2)

    def _gn(v, G=32, eps=1e-5):
        B_, C_, H_, W_ = v.shape
        g = v.reshape(B_, G, C_ // G, H_, W_)
        m = jnp.mean(g, axis=(2, 3, 4), keepdims=True)
        s = jnp.var(g, axis=(2, 3, 4), keepdims=True)
        return ((g - m) / jnp.sqrt(s + eps)).reshape(v.shape)

    def _ln_c(v, eps=1e-6):
        m = jnp.mean(v, axis=1, keepdims=True)
        s = jnp.var(v, axis=1, keepdims=True)
        return (v - m) / jnp.sqrt(s + eps)

    def _ln_t(v, eps=1e-5):
        m = jnp.mean(v, axis=-1, keepdims=True)
        s = jnp.var(v, axis=-1, keepdims=True)
        return (v - m) / jnp.sqrt(s + eps)

    def _to_tokens(v):
        B_, C_, H_, W_ = v.shape
        return v.reshape(B_, C_, H_ * W_).transpose(0, 2, 1)
    def _from_tokens(t, like):
        B_, C_, H_, W_ = like.shape
        return t.transpose(0, 2, 1).reshape(B_, C_, H_, W_)

    x = x + _L0_conv_ref(_gn(x), L0_conv_w_off, L0_conv_b_off, L0_conv_w_conv)
    x = x + _L1_conv_ref(_gn(x), L1_conv_w1, L1_conv_gamma1, L1_conv_beta1, L1_conv_w2, L1_conv_gamma2, L1_conv_beta2)
    return x


_drawn_inputs = setup_inputs


def setup_inputs(seed=0):
    import zlib

    import numpy as np

    out = dict(_drawn_inputs(seed))
    spreads = {'L0_conv_b_off': (0.0, 0.1),
     'L1_conv_gamma1': (1.0, 0.2),
     'L1_conv_beta1': (0.0, 0.1),
     'L1_conv_gamma2': (1.0, 0.2),
     'L1_conv_beta2': (0.0, 0.1)}
    factors = {}
    for name, (base, spread) in spreads.items():
        noise = np.random.default_rng([zlib.crc32(name.encode()), seed]).standard_normal(out[name].shape)
        drawn = base * np.exp(spread * noise) if base else spread * noise
        out[name] = jnp.asarray(drawn.astype(out[name].dtype))
    for name, factor in factors.items():
        out[name] = (out[name] * factor).astype(out[name].dtype)
    return out
```

```python
def build(nc, x, w_off, b_off, w_conv, w1, w2, bn_params, ident, group_avg, sel_hl, base, out):
    import concourse.bass as bass
    from concourse import mybir
    from contextlib import ExitStack

    F32, F32R, BF16, I32 = mybir.dt.float32, mybir.dt.float32r, mybir.dt.bfloat16, mybir.dt.int32
    ALU, ACT, AX = mybir.AluOpType, mybir.ActivationFunctionType, mybir.AxisListType
    ds = bass.ds

    NB, C, H, W = 4, 256, 64, 64
    CT = C // 128
    TAPS = 9
    RC = 8
    PX = RC * W
    NR = H // RC
    NCH = NB * NR
    PT = PX // 128
    NG = TAPS * PT
    RING = 9
    QP = 65
    NW = CT * TAPS * C
    EPS = 1e-5

    tbl = [nc.dram_tensor(f"quads{b}", (QP, QP, 4, C), F32).ap() for b in range(NB)]
    x1_d = nc.dram_tensor("x1", (NB, C, H, W), F32).ap()
    h1_d = nc.dram_tensor("h1", (NB, C, H, W), F32).ap()

    def rows_of(t, b, r0, n):
        v = t.rearrange("b (t c) h w -> b c t h w", c=128)
        return v[ds(b, 1), :, :, ds(r0, n), :].rearrange("b c t h w -> (b c) t (h w)")

    def flat(ap):
        return ap.rearrange("p t h w -> p t (h w)")

    outer = ExitStack()
    names = ExitStack()

    def sem(n):
        return names.enter_context(nc.semaphore(n))

    def need(eng, s, v):
        if not isinstance(v, int) or v > 0:
            eng.wait_ge(s, v)

    s_held = sem("held")

    def hold(eng, s, v):
        if isinstance(v, int) and v <= 0:
            return
        eng.wait_ge(s, v)
        eng.sem_inc(s_held, 1)

    def sb(stack, n, shape, dt=F32):
        return stack.enter_context(nc.sbuf_tensor(n, shape, dt))

    def ps(stack, n, shape, dt=F32):
        return stack.enter_context(nc.psum_tensor(n, shape, dt))

    with outer, names:
        q2b = sb(outer, "q2b", [128, CT, TAPS, C], BF16)
        bn1_stats = sb(outer, "bn1_stats", [128, CT, NCH, 6])
        gb = sb(outer, "gb", [128, 4, CT])
        eps_t = sb(outer, "eps_t", [128, 1])

        class Chunk:
            def __init__(self, b, r, r_half, p, first, last):
                self.b, self.r, self.p, self.first, self.last = b, r, p, first, last
                self.n, self.half = b * NR + r, b * (NR // 2) + r_half
                self.top = 1 if first else 0
                self.rows = 10 - (1 if first else 0) - (1 if last else 0)
                self.y0 = r * RC - (0 if first else 1)

        def walk(eng, emit):
            emit(0, 0, 0, True, False)
            with eng.Fori(0, NR // 2 - 1) as j:
                emit(2 * j + 1, j, 1, False, False)
                emit(2 * j + 2, j + 1, 0, False, False)
            emit(NR - 1, NR // 2 - 1, 1, False, True)

        one = ExitStack()
        with one:
            G = sb(one, "G", [128, RING, 4 * C])
            ST = sb(one, "ST", [128, 3, CT, PX])
            wconv = sb(one, "wconv", [128, CT, TAPS, C])
            woff = sb(one, "woff", [128, CT, TAPS, 64], F32R)
            q1 = sb(one, "q1", [128, CT, TAPS, C], F32R)
            xo = sb(one, "xo", [128, 2, CT, 10, W])
            xf = sb(one, "xf", [128, 2, CT, 10, W])
            po = sb(one, "po", [128, 2, 2, CT, 10, W + 2], F32R)
            pf = sb(one, "pf", [128, 2, 2, CT, 10, W + 2], F32R)
            yT = sb(one, "yT", [128, PT, C])
            om_c = sb(one, "om_c", [64, PX])
            om = sb(one, "om", [128, PT, 27])
            base_s = sb(one, "base_s", [128, NR, PT * 18])
            pos = sb(one, "pos", [128, 3, PT * 18])
            posi = sb(one, "posi", [128, PT * 18], I32)
            mk = sb(one, "mk", [128, 3, PT * TAPS])
            quad = sb(one, "quad", [128, NR, NG], I32)
            wts = sb(one, "wts", [128, NR, 4 * NG])
            quad_c = sb(one, "quad_c", [128, 2, NG], I32)
            wts_c = sb(one, "wts_c", [128, 2, 4 * NG])
            xres = sb(one, "xres", [128, 2, CT, PX])
            x1c = sb(one, "x1c", [128, CT, PX])
            h1c = sb(one, "h1c", [128, CT, PX])
            idn = sb(one, "idn", [128, 128])
            gavg = sb(one, "gavg", [128, 128])
            selhl = sb(one, "selhl", [64, 27])
            boff = sb(one, "boff", [64, 1])
            ones = sb(one, "ones", [128, 128])
            st0 = sb(one, "st0", [128, NB, CT, NR, 6])
            st1 = sb(one, "st1", [128, CT, NR, 6])
            mv = sb(one, "mv", [128, NB * CT, 2])
            gm = sb(one, "gm", [128, NB * CT, 2])
            gsq = sb(one, "gsq", [128, NB * CT])
            sc0 = sb(one, "sc0", [128, NB, CT])
            bi0 = sb(one, "bi0", [128, NB, CT])
            sc1 = sb(one, "sc1", [128, CT])
            bi1 = sb(one, "bi1", [128, CT])
            wst = sb(one, "wst", [128, 4])
            wmm = sb(one, "wmm", [2, 4])
            wall = sb(one, "wall", [128, 8])

            psA = ps(one, "psA", [128, 512])
            psX = ps(one, "psX", [128, 512])
            psT = ps(one, "psT", [128, CT, PX])
            psD = ps(one, "psD", [128, CT, PX])
            psF = ps(one, "psF", [128, CT, PX])
            ps_yT, ps_om, ps_gn, ps_w = psX[:, 0:C], psX[:, 256:256 + PT * 27], psX[:, 384:400], psX[:, 404:412]
            stage = G[:, 0:5, :].rearrange("p s c -> p (s c)")[:, 0:NW]
            stage_g = G[:, 5:9, :].rearrange("p s c -> p (s c)")
            raw_off = ST[:, 0, :, :].rearrange("p t x -> p (t x)")[:, 0:CT * TAPS * 27].rearrange(
                "p (t k j) -> p t k j", t=CT, k=TAPS)
            tmpq = wconv[:, :, :, :].rearrange("p t k o -> p (t k o)")
            zero_sb = xf[:, 0, :, :, :].rearrange("p t h w -> p (t h w)")[:, 0:2 * C]

            s_const, s_zero, s_edge, s_wraw = sem("const_loaded"), sem("zeros_set"), sem("edges_written"), sem("wraw_loaded")
            s_wconv = sem("wconv_loaded")
            s_sx = [sem(f"stat_x_loaded{i}") for i in range(2)]
            s_sxd = sem("stat_x_done")
            s_init = sem("init_steps")
            s_tern, s_wtr, s_wrd, s_wbc = sem("ternary_done"), sem("w_transposed"), sem("w_reduced"), sem("w_broadcast")
            s_woff = sem("woff_split")
            s_gnst, s_gnmm, s_gnv, s_gnsq, s_gnok = sem("gn_moments"), sem("gn_group_sums"), sem("gn_var"), sem("gn_sqrt"), sem("gn_ready")
            s_gch, s_gsum = sem("gn_step"), sem("gn_aggregated")
            CREDIT = 2
            o_load = [sem(f"o_x_loaded{i}") for i in range(2)]
            o_y, o_hi, o_split, o_conv = sem("o_y_ready"), sem("o_hi_ready"), sem("o_split_ready"), sem("o_conv_done")
            o_tr, o_yt, o_tw = sem("o_y_transposed"), sem("o_yT_ready"), sem("o_table_written")
            o_omc, o_om, o_sig, o_ix, o_idx = sem("o_om_evacuated"), sem("o_om_turned"), sem("o_om_ready"), sem("o_index_step"), sem("o_index_ready")
            d_pick, d_qpick = sem("d_weights_picked"), sem("d_rows_picked")
            d_g = [sem(f"d_gathered{i}") for i in range(RING)]
            d_m0, d_mac, d_tr, d_st, d_conv = sem("d_first_corner"), sem("d_mac_done"), sem("d_transposed"), sem("d_st_ready"), sem("d_conv_done")
            d_xl = [sem(f"d_xres_loaded{i}") for i in range(2)]
            d_x1, d_stat, d_store = sem("d_x1_ready"), sem("d_stats_done"), sem("d_x1_stored")
            f_load = [sem(f"f_x1_loaded{i}") for i in range(2)]
            f_y, f_hi, f_split, f_conv = sem("f_y_ready"), sem("f_hi_ready"), sem("f_split_ready"), sem("f_conv_done")
            f_h, f_stat, f_store = sem("f_h1_ready"), sem("f_stats_done"), sem("f_h1_stored")

            def schedule(eng, emit, tail=None):
                def slot(s, do_o, do_d, do_f):
                    def at(r, rh, p, first, last):
                        c = lambda b: Chunk(b, r, rh, p, first, last)
                        emit(s, c(s + 1) if do_o else None, c(s) if do_d else None, c(s - 1) if do_f else None)
                    walk(eng, at)
                slot(-1, True, False, False)
                slot(0, True, True, False)
                for s in range(1, NB - 1):
                    slot(s, True, True, True)
                slot(NB - 1, False, True, True)
                slot(NB, False, False, True)

            NSX = NB * NR
            O_TAPS = {2: [0, 1], 3: [2, 3], 4: [4, 5], 5: [6, 7], 6: [8]}
            F_TAPS = {4: [0, 1], 5: [2, 3], 6: [4, 5], 7: [6, 7], 8: [8]}
            IXS = 13

            block = one.enter_context(nc.Block())

            @block.sync
            def _(sp):
                for dst, src in ((idn[:], ident), (gavg[:], group_avg), (selhl[:], sel_hl),
                                 (base_s[:].rearrange("p r i -> p (r i)"), base.rearrange("p r i -> p (r i)")),
                                 (raw_off, w_off.rearrange("(t c) k j -> c t k j", c=128)),
                                 (gb[:], bn_params)):
                    sp.dma_start(dst, src).then_inc(s_const, 16)
                sp.wait_ge(s_zero, 2)
                sp.dma_start(boff[0:27, :], b_off.rearrange("(a o) -> a o", o=1)).then_inc(s_const, 16)
                xs = x.rearrange("b (t c) (r h) w -> b r c t (h w)", c=128, h=RC)
                for i in range(2):
                    sp.dma_start(stage_g[:, i * 1024:(i + 1) * 1024].rearrange("p (t x) -> p t x", t=CT),
                                 xs[0, i]).then_inc(s_sx[i], 16)
                sp.dma_start(stage, w1.rearrange("(t c) k o -> c t (k o)", c=128)).then_inc(s_wraw, 16)
                for n in range(2, NSX):
                    sp.wait_ge(s_sxd, n - 1)
                    sp.dma_start(stage_g[:, (n % 2) * 1024:(n % 2 + 1) * 1024].rearrange("p (t x) -> p t x", t=CT),
                                 xs[n // NR, n % NR]).then_inc(s_sx[n % 2], 16)
                edges = 0
                sp.wait_ge(s_zero, 6)
                for dsts in ([tbl[b][y, :, 2 * q:2 * q + 2, :].rearrange("x q c -> x (q c)")
                              for b in range(NB) for y, q in ((0, 0), (QP - 1, 1))],
                             [tbl[b][:, xx, q, :] for b in range(NB) for xx, q in ((0, 0), (0, 2), (QP - 1, 1), (QP - 1, 3))]):
                    need(sp, s_edge, 16 * edges)
                    for d in dsts:
                        sp.dma_start(d, zero_sb[0:QP, 0:d.shape[1]]).then_inc(s_edge, 16)
                        edges += 1
                sp.wait_ge(s_edge, 16 * edges)
                sp.wait_ge(s_tern, 1)
                sp.dma_start(stage, w2.rearrange("(t c) k o -> c t (k o)", c=128)).then_inc(s_wraw, 16)
                sp.wait_ge(s_tern, 2)
                sp.dma_start(wconv[:].rearrange("p t k o -> p t (k o)"),
                             w_conv.rearrange("(t c) k o -> c t (k o)", c=128)).then_inc(s_wconv, 16)
                sp.sem_inc(f_store, CREDIT)

                def store_x1(b, r, n):
                    hold(sp, d_x1, n + 1 + CREDIT)
                    sp.dma_start(rows_of(x1_d, b, r * RC, RC), x1c[:]).then_inc(d_store, 16)

                def emit(s, o, d, f):
                    if d:
                        hold(sp, d_x1, d.n - 1 + CREDIT)
                        sp.dma_start(xres[:, d.p], rows_of(x, d.b, d.r * RC, RC)).then_inc(d_xl[d.p], 16)
                    if o:
                        hold(sp, o_split, o.n - 1 + CREDIT)
                        hold(sp, o_tr, PT * (o.n - 1) + CREDIT)
                        sp.dma_start(flat(xo[:, o.p, :, o.top:o.top + o.rows, :]),
                                     rows_of(x, o.b, o.y0, o.rows)).then_inc(o_load[o.p], 16)
                    if d and not (isinstance(d.n, int) and d.n == 0):
                        if d.first:
                            store_x1(d.b - 1, NR - 1, d.n - 1)
                        else:
                            store_x1(d.b, d.r - 1, d.n - 1)
                    if f:
                        if f.first and isinstance(s, int) and s == NB:
                            store_x1(NB - 1, NR - 1, NCH - 1)
                        if f.first:
                            hold(sp, d_store, 16 * (f.n + NR))
                        hold(sp, f_split, f.n - 1 + CREDIT)
                        sp.dma_start(flat(xf[:, f.p, :, f.top:f.top + f.rows, :]),
                                     rows_of(x1_d, f.b, f.y0, f.rows)).then_inc(f_load[f.p], 16)
                    if o:
                        hold(sp, o_yt, PT * (o.n + 1))
                        for h in range(2):
                            for dy in range(2):
                                for dx in range(2):
                                    dst = tbl[o.b][ds(o.r * RC + h + 1 - dy, PT, step=2), 1 - dx:1 - dx + W, 2 * dy + dx, :]
                                    sp.dma_start(dst.rearrange("t x c -> x t c"),
                                                 yT[64 * h:64 * h + 64, :, :]).then_inc(o_tw, 16)
                    if f:
                        hold(sp, f_h, f.n + 1 + CREDIT)
                        sp.dma_start(rows_of(h1_d, f.b, f.r * RC, RC), h1c[:]).then_inc(f_store, 16)
                schedule(sp, emit)
                hold(sp, f_store, 16 * NCH + CREDIT)
                hold(sp, d_store, 16 * NCH)

            @block.gpsimd
            def _(pool):
                pool.memset(ones[:], 1.0).then_inc(s_zero, 1)
                pool.memset(boff[:], 0.0).then_inc(s_zero, 1)
                pool.memset(xf[:], 0.0).then_inc(s_zero, 1)
                pool.memset(po[:].bitcast(F32), 0.0).then_inc(s_zero, 1)
                pool.memset(pf[:].bitcast(F32), 0.0).then_inc(s_zero, 1)
                pool.memset(eps_t[:], EPS).then_inc(s_zero, 1)

                def emit(s, o, d, f):
                    if not d:
                        return
                    if d.first:
                        hold(pool, o_tw, 128 * (d.n + NR))
                    hold(pool, o_idx, d.n + 1)
                    hold(pool, d_tr, TAPS * (d.n - 1) + CREDIT)
                    pool.tensor_copy(quad_c[:, d.p, :], quad[:, ds(d.r, 1), :].rearrange("p r i -> p (r i)")).then_inc(d_qpick, 1)
                    hold(pool, d_qpick, d.n + 1)
                    for i in range(NG):
                        if i % PT == RING % PT:
                            hold(pool, d_tr, TAPS * d.n + (i - RING) // PT + 1 + CREDIT)
                        pool.indirect_dma_start(
                            out=G[:, i % RING, :], out_offset=None, in_=tbl[d.b].rearrange("y x q c -> (y x) (q c)"),
                            in_offset=bass.IndirectOffsetOnAxis(ap=quad_c[:, d.p, i:i + 1], axis=0)).then_inc(d_g[i % RING], 16)
                schedule(pool, emit)

            @block.scalar
            def _(act):
                act.wait_ge(s_zero, 6)
                act.wait_ge(s_woff, 1)
                act.wait_ge(s_gnv, 1)
                act.activation(gsq[:], gsq[:], ACT.Sqrt, bias=eps_t[:, 0:1]).then_inc(s_gnsq, 1)
                act.wait_ge(s_gnok, 1)
                act.wait_ge(s_const, 112)
                act.wait_ge(s_edge, 384)

                def emit(s, o, d, f):
                    for k in range(TAPS):
                        if f and f.first and k == 1:
                            act.wait_ge(s_gnv, f.b + 2)
                            act.activation(gsq[:, 0:CT], gsq[:, 0:CT], ACT.Sqrt, bias=eps_t[:, 0:1]).then_inc(s_gnsq, 1)
                        if d:
                            if k == 0:
                                act.wait_ge(d_pick, d.n + 1)
                            for t in range(PT):
                                i = PT * k + t
                                act.wait_ge(d_g[i % RING], 16 * (4 * d.n + i // RING + 1))
                                g = G[:, i % RING, 0:C]
                                act.activation(g, g, ACT.Copy, scale=wts_c[:, d.p, i:i + 1]).then_inc(d_m0, 1)
                            if k > 0:
                                st_evac(d, k - 1)
                        if o and k == 1:
                            hold(act, o_load[o.p], 16 * (o.half + 1))
                            for t in range(CT):
                                v = xo[:, o.p, t, o.top:o.top + o.rows, :]
                                i = act.activation(v, v, ACT.Identity, bias=bi0[:, ds(o.b, 1), t], scale=sc0[:, ds(o.b, 1), t])
                            i.then_inc(o_y, 1)
                        if o and 4 <= k < 4 + PT:
                            need(act, o_tr, PT * o.n + k - 3 + CREDIT)
                            if k == 4:
                                need(act, o_tw, 128 * o.n)
                            act.activation(yT[:, k - 4, :], ps_yT, ACT.Copy).then_inc(o_yt, 1)
                        if f and k == 3:
                            if f.first:
                                act.wait_ge(s_gnok, f.b + 2)
                            act.wait_ge(f_load[f.p], 16 * (f.half + 1))
                            for t in range(CT):
                                v = xf[:, f.p, t, f.top:f.top + f.rows, :]
                                i = act.activation(v, v, ACT.Identity, bias=bi1[:, t:t + 1], scale=sc1[:, t:t + 1])
                            i.then_inc(f_y, 1)
                    if o:
                        need(act, o_conv, o.n + 1 + CREDIT)
                        act.activation(om_c[:], psA[0:64, :], ACT.Identity, bias=boff[:, 0:1], scale=1.0).then_inc(o_omc, 1)
                    if d:
                        st_evac(d, TAPS - 1)
                    if f:
                        act.wait_ge(f_conv, f.n + 1 + CREDIT)
                        act.wait_ge(f_store, 16 * f.n + CREDIT)
                        act.wait_ge(f_stat, f.n + CREDIT)
                        act.activation(h1c[:], psF[:], ACT.Copy).then_inc(f_h, 1)
                    if o:
                        act.wait_ge(o_om, o.n + 1)
                        need(act, o_idx, o.n)
                        act.activation(om[:].rearrange("p t j -> p (t j)"), ps_om, ACT.Copy).then_inc(o_sig, 1)
                        act.activation(mk[:, 0, :].rearrange("p (t k) -> p t k", t=PT),
                                       ps_om.rearrange("p (t j) -> p t j", t=PT)[:, :, 18:27], ACT.Sigmoid).then_inc(o_sig, 1)

                def st_evac(d, k):
                    need(act, d_tr, TAPS * d.n + k + 1 + CREDIT)
                    need(act, d_conv, TAPS * d.n + k - 2)
                    act.activation(ST[:, k % 3], psT[:], ACT.Copy).then_inc(d_st, 1)

                for free in (f_h, d_m0):
                    act.sem_inc(free, CREDIT)
                schedule(act, emit)

            @block.vector
            def _(dve):
                count = [0]

                def step(ins):
                    ins.then_inc(s_init, 1)
                    count[0] += 1
                    dve.wait_ge(s_init, count[0])

                dve.wait_ge(s_const, 112)
                dve.wait_ge(s_zero, 6)
                step(dve.memset(woff[:].bitcast(F32), 0.0))
                step(dve.tensor_copy(woff[:, :, :, 0:27], raw_off))
                for t in range(CT):
                    i = dve.tensor_tensor(woff[:, t, :, 32:59], raw_off[:, t], woff[:, t, :, 0:27].bitcast(F32), ALU.subtract)
                i.then_inc(s_woff, 1)

                def ternary(m, raw, q):
                    dve.wait_ge(s_wraw, 16 * (m + 1))
                    dve.tensor_reduce(wst[:, 0:1], raw, AX.X, ALU.add)
                    dve.tensor_reduce(wst[:, 1:2], raw, AX.X, ALU.max)
                    step(dve.tensor_reduce(wst[:, 2:3], raw, AX.X, ALU.min))
                    dve.tensor_scalar(wst[:, 2:3], wst[:, 2:3], -1.0, None, ALU.mult).then_inc(s_wtr, 1)
                    dve.wait_ge(s_wrd, 2 * m + 1)
                    step(dve.tensor_reduce(wmm[:, 0:1], ps_w_row, AX.X, ALU.max))
                    dve.tensor_scalar(wmm[:, 1:3], idn[0:2, 0:2], wmm[:, 0:1], None, ALU.mult).then_inc(s_wtr, 1)
                    dve.wait_ge(s_wrd, 2 * m + 2)
                    step(dve.tensor_copy(wall[:, 0:3], ps_w[:, 0:3]))
                    step(dve.tensor_scalar(wall[:, 3:4], wall[:, 0:1], 1.0 / (C * C * TAPS), None, ALU.mult))
                    step(dve.tensor_tensor(wall[:, 1:2], wall[:, 1:2], wall[:, 3:4], ALU.subtract))
                    step(dve.scalar_tensor_tensor(wall[:, 2:3], wall[:, 2:3], -1.0, wall[:, 3:4], ALU.mult, ALU.subtract))
                    step(dve.tensor_tensor(wall[:, 4:5], wall[:, 1:2], wall[:, 2:3], ALU.subtract))
                    step(dve.tensor_scalar(wall[:, 4:5], wall[:, 4:5], 1.0 / 3.0, None, ALU.mult))
                    step(dve.tensor_tensor(wall[:, 5:6], wall[:, 2:3], wall[:, 4:5], ALU.add))
                    step(dve.tensor_tensor(wall[:, 6:7], wall[:, 1:2], wall[:, 4:5], ALU.subtract))
                    step(dve.tensor_scalar(tmpq, raw, wall[:, 3:4], wall[:, 6:7], ALU.subtract, ALU.is_gt))
                    step(dve.tensor_scalar(raw, raw, wall[:, 3:4], wall[:, 5:6], ALU.subtract, ALU.is_lt))
                    dve.tensor_tensor(q, tmpq, raw, ALU.subtract).then_inc(s_tern, 1)

                ps_w_row = psX[0:2, 0:128]
                ternary(0, stage, q1[:].rearrange("p t k o -> p (t k o)"))
                for n in range(NSX):
                    dve.wait_ge(s_sx[n % 2], 16 * (n // 2 + 1))
                    for t in range(CT):
                        i = dve.bn_stats(st0[:, n // NR, t, n % NR, :],
                                         stage_g[:, (n % 2) * 1024 + t * 512:(n % 2) * 1024 + (t + 1) * 512])
                    i.then_inc(s_sxd, 1)
                dve.wait_ge(s_sxd, NSX)
                for i in range(NB * CT):
                    ins = dve.bn_aggr(mv[:, i, :], st0[:, i // CT, i % CT].rearrange("p r s -> p (r s)"))
                step(ins)

                GS = 5

                def group_norm(c, k, scale, bias):
                    mean, var = mv[:, 0:k, 0], mv[:, 0:k, 1]
                    dve.tensor_tensor(gsq[:, 0:k], mean, mean, ALU.mult).then_inc(s_gch, 1)
                    dve.wait_ge(s_gch, GS * c + 1)
                    dve.tensor_tensor(var, var, gsq[:, 0:k], ALU.add).then_inc(s_gnst, 1)
                    dve.wait_ge(s_gnmm, c + 1)
                    dve.tensor_copy(gm[:, 0:k, :].rearrange("p k m -> p (k m)"), ps_gn[:, 0:2 * k]).then_inc(s_gch, 1)
                    dve.wait_ge(s_gch, GS * c + 2)
                    dve.tensor_tensor(gsq[:, 0:k], gm[:, 0:k, 0], gm[:, 0:k, 0], ALU.mult).then_inc(s_gch, 1)
                    dve.wait_ge(s_gch, GS * c + 3)
                    dve.tensor_tensor(gsq[:, 0:k], gm[:, 0:k, 1], gsq[:, 0:k], ALU.subtract).then_inc(s_gch, 1)
                    dve.wait_ge(s_gch, GS * c + 4)
                    dve.tensor_scalar(gsq[:, 0:k], gsq[:, 0:k], 0.0, None, ALU.max).then_inc(s_gnv, 1)
                    dve.wait_ge(s_gnsq, c + 1)
                    dve.reciprocal(scale, gsq[:, 0:k]).then_inc(s_gch, 1)
                    dve.wait_ge(s_gch, GS * c + 5)
                    dve.scalar_tensor_tensor(bias, gm[:, 0:k, 0], -1.0, scale, ALU.mult, ALU.mult).then_inc(s_gnok, 1)

                group_norm(0, NB * CT, sc0[:].rearrange("p b t -> p (b t)"), bi0[:].rearrange("p b t -> p (b t)"))
                ternary(1, stage, q2b[:].rearrange("p t k o -> p (t k o)"))

                def split(c, src, pad, y, hi, done, conv):
                    dve.wait_ge(y, c.n + 1)
                    dve.wait_ge(conv, c.n - 1 + CREDIT)
                    rows = slice(c.top, c.top + c.rows)
                    for t in range(CT):
                        i = dve.tensor_copy(pad[:, c.p, 0, t, rows, 1:W + 1], src[:, c.p, t, rows, :])
                    i.then_inc(hi, 1)
                    if c.first or c.last:
                        edge = 0 if c.first else 9
                        for part in range(2):
                            dve.memset(pad[:, c.p, part, :, edge, 1:W + 1].bitcast(F32), 0.0)
                    dve.wait_ge(hi, c.n + 1)
                    for t in range(CT):
                        i = dve.tensor_tensor(pad[:, c.p, 1, t, rows, 1:W + 1], src[:, c.p, t, rows, :],
                                              pad[:, c.p, 0, t, rows, 1:W + 1].bitcast(F32), ALU.subtract)
                    i.then_inc(done, 1)

                def finish_deform(b, r, n, p, half):
                    dve.wait_ge(d_conv, TAPS * (n + 1))
                    dve.wait_ge(d_xl[p], 16 * (half + 1))
                    need(dve, d_store, 16 * n)
                    dve.tensor_tensor(x1c[:], psD[:], xres[:, p], ALU.add).then_inc(d_x1, 1)
                    need(dve, d_x1, n + 1 + CREDIT)
                    for t in range(CT):
                        i = dve.bn_stats(st1[:, t, ds(r, 1), :].rearrange("p r s -> p (r s)"), x1c[:, t, :])
                    i.then_inc(d_stat, 1)

                def gn1(b):
                    hold(dve, d_stat, NR * (b + 1))
                    for t in range(CT):
                        ins = dve.bn_aggr(mv[:, t, :], st1[:, t].rearrange("p r s -> p (r s)"))
                    ins.then_inc(s_gsum, 1)
                    dve.wait_ge(s_gsum, b + 1)
                    group_norm(b + 1, CT, sc1[:], bi1[:])

                def indices(o):
                    c0 = [IXS * o.n]

                    def go(ins):
                        ins.then_inc(o_ix, 1)
                        c0[0] = c0[0] + 1
                        dve.wait_ge(o_ix, c0[0])
                    P, Fl, Lf = (pos[:, i, :] for i in range(3))
                    v3 = lambda a: a.rearrange("p (t i) -> p t i", t=PT)
                    yx = lambda a, m: a.rearrange("p (t k m) -> p k t m", t=PT, m=2)[:, :, :, m]
                    kt = lambda a: a.rearrange("p (k t) -> p k t", t=PT)
                    w4 = wts[:, ds(o.r, 1), :].rearrange("p r (q i) -> p (r q) i", q=4)
                    dve.wait_ge(o_sig, 2 * (o.n + 1))
                    go(dve.tensor_tensor(v3(P), om[:, :, 0:18], v3(base_s[:, ds(o.r, 1), :].rearrange("p r i -> p (r i)")), ALU.add))
                    go(dve.tensor_scalar(P, P, 0.0, float(H + 1), ALU.max, ALU.min))
                    go(dve.tensor_copy(posi[:], P))
                    go(dve.tensor_copy(Fl, posi[:]))
                    go(dve.tensor_tensor(Lf, Fl, P, ALU.is_gt))
                    go(dve.tensor_tensor(Fl, Fl, Lf, ALU.subtract))
                    go(dve.tensor_scalar(Fl, Fl, float(H), None, ALU.min))
                    go(dve.tensor_tensor(Lf, P, Fl, ALU.subtract))
                    go(dve.tensor_scalar(P, Lf, -1.0, 1.0, ALU.mult, ALU.add))
                    m9 = mk[:, 0, :].rearrange("p (t k) -> p k t", t=PT)
                    go(dve.tensor_tensor(kt(mk[:, 1, :]), m9, yx(P, 0), ALU.mult))
                    go(dve.tensor_tensor(kt(mk[:, 2, :]), m9, yx(Lf, 0), ALU.mult))
                    for q in range(4):
                        ins = dve.tensor_tensor(kt(w4[:, q, :]), kt(mk[:, 1 + q // 2, :]), yx((P, Lf)[q % 2], 1), ALU.mult)
                    go(ins)
                    go(dve.scalar_tensor_tensor(kt(mk[:, 1, :]), yx(Fl, 0), float(QP), yx(Fl, 1), ALU.mult, ALU.add))
                    if not (isinstance(o.b, int) and o.b == 0):
                        dve.wait_ge(d_qpick, o.n - NR + 1)
                    dve.tensor_copy(quad[:, ds(o.r, 1), :].rearrange("p r i -> p (r i)"), mk[:, 1, :]).then_inc(o_idx, 1)

                def emit(s, o, d, f):
                    if d:
                        need(dve, d_mac, 3 * NG * (d.n - 1) + CREDIT)
                        need(dve, d_m0, NG * (d.n - 1) + CREDIT)
                        dve.tensor_copy(wts_c[:, d.p, :], wts[:, ds(d.r, 1), :].rearrange("p r i -> p (r i)")).then_inc(d_pick, 1)
                        dve.wait_ge(d_pick, d.n + 1)
                    for k in range(TAPS):
                        if d:
                            for q in range(1, 4):
                                for t in range(PT):
                                    i = PT * k + t
                                    g = G[:, i % RING, :]
                                    if q == 1:
                                        need(dve, d_m0, NG * d.n + i + 1 + CREDIT)
                                    else:
                                        need(dve, d_mac, 3 * NG * d.n + 3 * PT * k + PT * (q - 2) + t + 1 + CREDIT)
                                    dve.scalar_tensor_tensor(g[:, 0:C], g[:, q * C:(q + 1) * C], wts_c[:, d.p, q * NG + i:q * NG + i + 1],
                                                             g[:, 0:C], ALU.mult, ALU.add).then_inc(d_mac, 1)
                            if k == 0:
                                if d.first:
                                    if not isinstance(d.b, int) or d.b > 0:
                                        finish_deform(d.b - 1, NR - 1, d.n - 1, 1, d.half - 1)
                                        gn1(d.b - 1)
                                else:
                                    finish_deform(d.b, d.r - 1, d.n - 1, 1 - d.p, d.half if d.p else d.half - 1)
                        elif k == 0 and f and f.first and isinstance(s, int) and s == NB:
                            finish_deform(NB - 1, NR - 1, NCH - 1, 1, NCH // 2 - 1)
                            gn1(NB - 1)
                        if o and k == 1:
                            split(o, xo, po, o_y, o_hi, o_split, o_conv)
                        if f and k == 3:
                            split(f, xf, pf, f_y, f_hi, f_split, f_conv)
                    if f:
                        dve.wait_ge(f_h, f.n + 1 + CREDIT)
                        for t in range(CT):
                            ins = dve.bn_stats(bn1_stats[:, t, ds(f.n, 1), :].rearrange("p r s -> p (r s)"), h1c[:, t, :])
                        ins.then_inc(f_stat, 1)
                    if o:
                        indices(o)
                for free in (f_split, o_split, d_x1, d_mac):
                    dve.sem_inc(free, CREDIT)
                dve.sem_inc(f_stat, CREDIT)
                schedule(dve, emit)

            @block.tensor
            def _(pe):
                pe.wait_ge(s_zero, 6)
                pe.wait_ge(s_const, 112)

                def weight_extremes(m):
                    pe.wait_ge(s_wtr, 2 * m + 1)
                    pe.transpose(psX[0:2, 0:128], wst[:, 1:3], idn[:]).then_inc(s_wrd, 1)
                    pe.wait_ge(s_wtr, 2 * m + 2)
                    pe.matmul(ps_w[:, 0:1], ones[:], wst[:, 0:1], start=True, stop=True)
                    pe.matmul(ps_w[:, 1:3], ones[0:2, :], wmm[:, 1:3], start=True, stop=True).then_inc(s_wrd, 1)

                def group_sums(c, k):
                    pe.wait_ge(s_gnst, c + 1)
                    pe.matmul(ps_gn[:, 0:2 * k], gavg[:], mv[:, 0:k, :].rearrange("p k m -> p (k m)"), start=True, stop=True).then_inc(s_gnmm, 1)

                weight_extremes(0)
                group_sums(0, NB * CT)
                weight_extremes(1)
                pe.wait_ge(s_woff, 1)
                pe.wait_ge(s_tern, 2)
                pe.wait_ge(s_wconv, 16)

                def conv_tap(c, pad, w, acc, tap, first, last, m):
                    dy, dx = tap // 3, tap % 3
                    for oc in range(acc.shape[1]):
                        for t in range(CT):
                            for part in range(2):
                                ins = pe.matmul(acc[:, oc, :].rearrange("p (h w) -> p h w", h=RC), w[:, t, tap, oc * m:(oc + 1) * m],
                                                pad[:, c.p, part, t, dy:dy + RC, dx:dx + W],
                                                start=(first and t == 0 and part == 0), stop=(last and t == CT - 1 and part == 1))
                    return ins

                def deform_tap(d, k):
                    pe.wait_ge(d_st, TAPS * d.n + k + 1)
                    if k == 0:
                        need(pe, d_x1, d.n + CREDIT)
                    for oc in range(CT):
                        for t in range(CT):
                            ins = pe.matmul(psD[:, oc, :], wconv[:, t, k, oc * 128:(oc + 1) * 128], ST[:, k % 3, t, :],
                                            start=(k == 0 and t == 0), stop=(k == TAPS - 1 and t == CT - 1))
                    ins.then_inc(d_conv, 1)

                def emit(s, o, d, f):
                    for k in range(TAPS):
                        if f and f.first and k == 1:
                            group_sums(s, CT)
                        if d:
                            need(pe, d_mac, 3 * NG * d.n + 3 * PT * (k + 1) + CREDIT)
                            need(pe, d_st, TAPS * d.n + k)
                            for t in range(PT):
                                for c in range(CT):
                                    ins = pe.transpose(psT[:, c, t * 128:(t + 1) * 128],
                                                       G[:, (PT * k + t) % RING, c * 128:(c + 1) * 128], idn[:])
                            ins.then_inc(d_tr, 1)
                            if k > 0:
                                deform_tap(d, k - 1)
                        if o:
                            for tap in O_TAPS.get(k, []):
                                if tap == 0:
                                    need(pe, o_split, o.n + 1 + CREDIT)
                                    need(pe, o_omc, o.n)
                                ins = conv_tap(o, po, woff, psA[0:64, :].rearrange("p (o x) -> p o x", o=1), tap, tap == 0, tap == TAPS - 1, 64)
                                if tap == TAPS - 1:
                                    ins.then_inc(o_conv, 1)
                            if 3 <= k < 3 + PT:
                                need(pe, o_yt, PT * o.n + k - 3)
                                for c in range(CT):
                                    ins = pe.transpose(ps_yT[:, c * 128:(c + 1) * 128],
                                                       xo[:, o.p, c, 1 + 2 * (k - 3):3 + 2 * (k - 3), :].rearrange("p h w -> p (h w)"), idn[:])
                                ins.then_inc(o_tr, 1)
                        if f:
                            for tap in F_TAPS.get(k, []):
                                if tap == 0:
                                    pe.wait_ge(f_split, f.n + 1 + CREDIT)
                                    pe.wait_ge(f_h, f.n + CREDIT)
                                ins = conv_tap(f, pf, q1, psF, tap, tap == 0, tap == TAPS - 1, 128)
                                if tap == TAPS - 1:
                                    ins.then_inc(f_conv, 1)
                    if d:
                        deform_tap(d, TAPS - 1)
                    if o:
                        pe.wait_ge(o_omc, o.n + 1)
                        need(pe, o_sig, 2 * o.n)
                        for t in range(PT):
                            ins = pe.matmul(ps_om[:, t * 27:(t + 1) * 27], om_c[:, t * 128:(t + 1) * 128], selhl[:], start=True, stop=True)
                        ins.then_inc(o_om, 1)
                for free in (f_conv, o_conv, o_tr, d_tr):
                    pe.sem_inc(free, CREDIT)
                schedule(pe, emit)

        two = ExitStack()
        names2 = ExitStack()
        with two, names2:
            def sem2(n):
                return names2.enter_context(nc.semaphore(n))

            h2 = sb(two, "h2", [128, CT, NCH * PX])
            q2 = sb(two, "q2", [128, CT, TAPS, C], F32R)
            work = sb(two, "work", [128, 6, CT * PX])
            pg = sb(two, "pg", [128, 2, 2, CT, 10, W + 2], F32R)
            flat_work = work[:].rearrange("p s x -> p (s x)")
            XN = 2 * CT * 10 * W
            xg = flat_work[:, 0:XN].rearrange("p (q t h w) -> p q t h w", q=2, t=CT, h=10)
            bn2_stats = sb(two, "bn2_stats", [128, CT, NCH, 6])
            mv2 = sb(two, "mv2", [128, CT, 2])
            sq = sb(two, "sq", [128, CT])
            scale_b = sb(two, "scale_b", [128, 2, CT])
            bias_b = sb(two, "bias_b", [128, 2, CT])
            psG = ps(two, "psG", [128, 2, CT, PX])

            g_q, g_zero, g_ag, g_sq, g_bn, g_bch = (sem2(n) for n in ("q2_ready", "borders_zero", "bn_moments", "bn_sqrt", "bn_ready", "bn_step"))
            g_load = [sem2(f"g_h1_loaded{i}") for i in range(2)]
            g_y, g_hi, g_split, g_conv, g_h, g_stat = (sem2(n) for n in ("g_y", "g_hi", "g_split", "g_conv", "g_h2", "g_stats"))
            e_lx = [sem2(f"e_x1_loaded{i}") for i in range(2)]
            e_lh = [sem2(f"e_h1_loaded{i}") for i in range(4)]
            e_st = [sem2(f"e_out_stored{i}") for i in range(4)]
            e_r1, e_mac, e_r2, e_sum = (sem2(n) for n in ("e_relu1", "e_mixed", "e_relu2", "e_out_ready"))
            CR = 2

            def batches(eng, emit):
                with eng.Fori(0, NB) as b:
                    walk(eng, lambda r, rh, p, first, last: emit(Chunk(b, r, rh, p, first, last)))

            block2 = two.enter_context(nc.Block())

            @block2.sync
            def _(sp):
                def emit(c):
                    hold(sp, g_split, c.n - 1 + CR)
                    sp.dma_start(flat(xg[:, c.p, :, c.top:c.top + c.rows, :]), rows_of(h1_d, c.b, c.y0, c.rows)).then_inc(g_load[c.p], 16)
                batches(sp, emit)
                hold(sp, g_conv, NCH + CR)

                def load_four(j):
                    for u in range(4):
                        b, r = j // 2, 4 * (j % 2) + u
                        hold(sp, e_st[u], 16 * j)
                        sp.dma_start(work[:, u, :].rearrange("p (t x) -> p t x", t=CT), rows_of(h1_d, b, r * RC, RC)).then_inc(e_lh[u], 16)
                        hold(sp, e_sum, 4 * j + u - 1 + CR)
                        sp.dma_start(work[:, 4 + u % 2, :].rearrange("p (t x) -> p t x", t=CT), rows_of(x1_d, b, r * RC, RC)).then_inc(e_lx[u % 2], 16)
                load_four(0)
                with sp.Fori(1, NCH // 4) as j:
                    load_four(j)

            @block2.gpsimd
            def _(pool):
                pool.memset(pg[:].bitcast(F32), 0.0).then_inc(g_zero, 1)

                def emit(c):
                    hold(pool, g_hi, c.n + 1)
                    rows = slice(c.top, c.top + c.rows)
                    if c.first or c.last:
                        edge = 0 if c.first else 9
                        for t in range(CT):
                            pool.memset(pg[:, c.p, 1, t, edge, 1:W + 1].bitcast(F32), 0.0)
                            pool.memset(pg[:, c.p, 0, t, edge, 1:W + 1].bitcast(F32), 0.0)
                    for t in range(CT):
                        i = pool.tensor_tensor(pg[:, c.p, 1, t, rows, 1:W + 1], xg[:, c.p, t, rows, :],
                                               pg[:, c.p, 0, t, rows, 1:W + 1].bitcast(F32), ALU.subtract)
                    i.then_inc(g_split, 1)
                pool.sem_inc(g_split, CR)
                batches(pool, emit)
                with pool.Fori(0, NCH // 4) as j:
                    for u in range(4):
                        hold(pool, e_sum, 4 * j + u + 1 + CR)
                        pool.dma_start(rows_of(out, j // 2, (4 * (j % 2) + u) * RC, RC),
                                       work[:, u, :].rearrange("p (t x) -> p t x", t=CT)).then_inc(e_st[u], 16)
                for u in range(4):
                    hold(pool, e_st[u], 16 * (NCH // 4))

            @block2.scalar
            def _(act):
                act.wait_ge(g_ag, 1)
                act.activation(sq[:], sq[:], ACT.Sqrt, bias=eps_t[:, 0:1]).then_inc(g_sq, 1)
                act.wait_ge(g_bn, 1)
                act.wait_ge(g_zero, 1)

                def emit(c):
                    act.wait_ge(g_load[c.p], 16 * (c.half + 1))
                    act.wait_ge(g_conv, c.n - 1 + CR)
                    rows = slice(c.top, c.top + c.rows)
                    for t in range(CT):
                        act.activation(pg[:, c.p, 0, t, rows, 1:W + 1], xg[:, c.p, t, rows, :], ACT.Relu,
                                       bias=bias_b[:, 0, t:t + 1], scale=scale_b[:, 0, t:t + 1])
                    for t in range(CT):
                        i = act.activation(xg[:, c.p, t, rows, :], xg[:, c.p, t, rows, :], ACT.Relu,
                                           bias=bias_b[:, 0, t:t + 1], scale=scale_b[:, 0, t:t + 1])
                    i.then_inc(g_hi, 1)
                batches(act, emit)
                act.wait_ge(g_ag, 2)
                act.activation(sq[:], sq[:], ACT.Sqrt, bias=eps_t[:, 0:1]).then_inc(g_sq, 1)
                act.wait_ge(g_bn, 2)
                with act.Fori(0, NCH // 4) as j:
                    def relu1(u):
                        act.wait_ge(e_lh[u], 16 * (j + 1))
                        for t in range(CT):
                            v = work[:, u, t * PX:(t + 1) * PX]
                            i = act.activation(v, v, ACT.Relu, bias=bias_b[:, 0, t:t + 1], scale=scale_b[:, 0, t:t + 1])
                        i.then_inc(e_r1, 1)

                    def relu2(u):
                        act.wait_ge(e_mac, 4 * j + u + 1)
                        for t in range(CT):
                            v = work[:, u, t * PX:(t + 1) * PX]
                            i = act.activation(v, v, ACT.Relu, bias=bias_b[:, 1, t:t + 1], scale=1.0)
                        i.then_inc(e_r2, 1)
                    relu1(0)
                    for u in range(1, 4):
                        relu1(u)
                        relu2(u - 1)
                    relu2(3)

            @block2.vector
            def _(dve):
                def batch_norm(m, stats):
                    for t in range(CT):
                        i = dve.bn_aggr(mv2[:, t, :], stats[:, t].rearrange("p n s -> p (n s)"))
                    i.then_inc(g_bch, 1)
                    dve.wait_ge(g_bch, 4 * m + 1)
                    dve.tensor_copy(sq[:], mv2[:, :, 1]).then_inc(g_ag, 1)
                    dve.wait_ge(g_sq, m + 1)
                    dve.reciprocal(sq[:], sq[:]).then_inc(g_bch, 1)
                    dve.wait_ge(g_bch, 4 * m + 2)
                    dve.tensor_tensor(scale_b[:, m, :], sq[:], gb[:, 2 * m, :], ALU.mult).then_inc(g_bch, 1)
                    dve.wait_ge(g_bch, 4 * m + 3)
                    dve.tensor_tensor(bias_b[:, m, :], mv2[:, :, 0], scale_b[:, m, :], ALU.mult).then_inc(g_bch, 1)
                    dve.wait_ge(g_bch, 4 * m + 4)
                    dve.tensor_tensor(bias_b[:, m, :], gb[:, 2 * m + 1, :], bias_b[:, m, :], ALU.subtract).then_inc(g_bn, 1)

                batch_norm(0, bn1_stats)
                dve.tensor_copy(q2[:].rearrange("p t k o -> p (t k o)"), q2b[:].rearrange("p t k o -> p (t k o)")).then_inc(g_q, 1)

                def emit(c):
                    dve.wait_ge(g_conv, c.n + 1 + CR)
                    dst = h2[:, :, ds(c.n * PX, PX)]
                    dve.tensor_copy(dst, psG[:, c.p]).then_inc(g_h, 1)
                    for t in range(CT):
                        i = dve.bn_stats(bn2_stats[:, t, ds(c.n, 1), :].rearrange("p r s -> p (r s)"), psG[:, c.p, t, :])
                    i.then_inc(g_stat, 1)
                dve.sem_inc(g_stat, CR)
                dve.sem_inc(e_sum, CR)
                batches(dve, emit)
                dve.wait_ge(g_stat, NCH + CR)
                dve.wait_ge(g_h, NCH)
                batch_norm(1, bn2_stats)
                with dve.Fori(0, NCH // 4) as j:
                    def mix(u):
                        dve.wait_ge(e_r1, 4 * j + u + 1)
                        for t in range(CT):
                            v = work[:, u, t * PX:(t + 1) * PX]
                            i = dve.scalar_tensor_tensor(v, h2[:, t, ds((4 * j + u) * PX, PX)], scale_b[:, 1, t:t + 1], v, ALU.mult, ALU.add)
                        i.then_inc(e_mac, 1)

                    def add_x1(u):
                        dve.wait_ge(e_r2, 4 * j + u + 1)
                        dve.wait_ge(e_lx[u % 2], 32 * j + 16 * (u // 2) + 16)
                        dve.tensor_tensor(work[:, u, :], work[:, u, :], work[:, 4 + u % 2, :], ALU.add).then_inc(e_sum, 1)
                    mix(0)
                    for u in range(1, 4):
                        mix(u)
                        add_x1(u - 1)
                    add_x1(3)

            @block2.tensor
            def _(pe):
                pe.wait_ge(g_q, 1)

                def emit(c):
                    pe.wait_ge(g_split, c.n + 1 + CR)
                    pe.wait_ge(g_stat, c.n - 1 + CR)
                    for tap in range(TAPS):
                        dy, dx = tap // 3, tap % 3
                        for oc in range(CT):
                            for t in range(CT):
                                for part in range(2):
                                    i = pe.matmul(psG[:, c.p, oc, :].rearrange("p (h w) -> p h w", h=RC), q2[:, t, tap, oc * 128:(oc + 1) * 128],
                                                  pg[:, c.p, part, t, dy:dy + RC, dx:dx + W],
                                                  start=(tap == 0 and t == 0 and part == 0),
                                                  stop=(tap == TAPS - 1 and t == CT - 1 and part == 1))
                    i.then_inc(g_conv, 1)
                pe.sem_inc(g_conv, CR)
                batches(pe, emit)


def kernel(x, L0_conv_w_off, L0_conv_b_off, L0_conv_w_conv, L1_conv_w1, L1_conv_gamma1, L1_conv_beta1,
           L1_conv_w2, L1_conv_gamma2, L1_conv_beta2):
    import numpy as np
    import concourse.bacc as bacc
    from concourse import mybir
    from concourse.bass_utils import run_bass_kernel_spmd as run

    def by_input(w):
        w = np.asarray(w)
        return np.ascontiguousarray(w.reshape(w.shape[0], w.shape[1], 9).transpose(1, 2, 0))

    eye = np.eye(128, dtype=np.float32)
    group = np.kron(np.eye(16, dtype=np.float32), np.full((8, 8), 1 / 8, np.float32))
    sel = np.zeros((64, 27), np.float32)
    sel[np.arange(27), np.arange(27)] = 1
    sel[32 + np.arange(27), np.arange(27)] = 1
    p, r, t, k = np.ix_(np.arange(128), np.arange(8), np.arange(4), np.arange(9))
    grid = np.stack([8 * r + 2 * t + p // 64 + k // 3, p % 64 + k % 3 + 0 * (r + t)], axis=-1)
    grid = np.ascontiguousarray(grid.reshape(128, 8, 72).astype(np.float32))

    params = np.stack([np.asarray(v) for v in (L1_conv_gamma1, L1_conv_beta1, L1_conv_gamma2, L1_conv_beta2)])
    params = np.ascontiguousarray(params.reshape(4, 2, 128).transpose(2, 0, 1))

    ins = {"x": np.asarray(x), "w_off": by_input(L0_conv_w_off), "b_off": np.asarray(L0_conv_b_off),
           "w_conv": by_input(L0_conv_w_conv), "w1": by_input(L1_conv_w1), "w2": by_input(L1_conv_w2),
           "bn_params": params, "ident": eye, "group_avg": group, "sel_hl": sel, "base": grid}
    nc = bacc.Bacc("TRN2", target_bir_lowering=False, num_devices=1)
    args = [nc.dram_tensor(f"in_{n}", a.shape, mybir.dt.from_np(a.dtype), kind="ExternalInput").ap() for n, a in ins.items()]
    args.append(nc.dram_tensor("out", (4, 256, 64, 64), mybir.dt.float32, kind="ExternalOutput").ap())
    build(nc, *args)
    r = run(nc, [{f"in_{n}": a for n, a in ins.items()}], core_ids=[0])
    return r.results[0]["out"]
```

```python
def build(nc, x, w_off, b_off, w_conv, w1, w2, bn_params, ident, group_avg, sel_hl, base, out):
    import concourse.bass as bass
    from concourse import mybir
    from contextlib import ExitStack

    F32, F32R, BF16, I32 = mybir.dt.float32, mybir.dt.float32r, mybir.dt.bfloat16, mybir.dt.int32
    ALU, ACT, AX = mybir.AluOpType, mybir.ActivationFunctionType, mybir.AxisListType
    ds = bass.ds

    NB, C, H, W = 4, 256, 64, 64
    CT = C // 128
    TAPS = 9
    RC = 8
    PX = RC * W
    NR = H // RC
    NCH = NB * NR
    PT = PX // 128
    NG = TAPS * PT
    RING = 12
    QP = 65
    NW = CT * TAPS * C
    EPS = 1e-5

    tbl = [nc.dram_tensor(f"quads{b}", (QP, QP, 4, C), F32).ap() for b in range(NB)]
    x1_d = nc.dram_tensor("x1", (NB, C, H, W), F32).ap()
    h1_d = nc.dram_tensor("h1", (NB, C, H, W), F32).ap()

    def rows_of(t, b, r0, n):
        v = t.rearrange("b (t c) h w -> b c t h w", c=128)
        return v[ds(b, 1), :, :, ds(r0, n), :].rearrange("b c t h w -> (b c) t (h w)")

    def flat(ap):
        return ap.rearrange("p t h w -> p t (h w)")

    outer = ExitStack()
    names = ExitStack()

    def sem(n):
        return names.enter_context(nc.semaphore(n))

    def need(eng, s, v):
        if not isinstance(v, int) or v > 0:
            eng.wait_ge(s, v)

    s_held = sem("held")

    def hold(eng, s, v):
        if isinstance(v, int) and v <= 0:
            return
        eng.wait_ge(s, v)
        eng.sem_inc(s_held, 1)

    def sb(stack, n, shape, dt=F32):
        return stack.enter_context(nc.sbuf_tensor(n, shape, dt))

    def ps(stack, n, shape, dt=F32):
        return stack.enter_context(nc.psum_tensor(n, shape, dt))

    with outer, names:
        qw = sb(outer, "qw", [128, CT, TAPS, C], F32R)
        bn1_stats = sb(outer, "bn1_stats", [128, CT, NCH, 6])
        gb = sb(outer, "gb", [128, 4, CT])
        eps_t = sb(outer, "eps_t", [128, 1])

        class Chunk:
            def __init__(self, b, r, r_half, p, first, last):
                self.b, self.r, self.p, self.first, self.last = b, r, p, first, last
                self.n, self.half = b * NR + r, b * (NR // 2) + r_half
                self.top = 1 if first else 0
                self.rows = 10 - (1 if first else 0) - (1 if last else 0)
                self.y0 = r * RC - (0 if first else 1)

            def after(self):
                return Chunk(self.b, self.r + 1, self.half - self.b * (NR // 2) + self.p, 1 - self.p, False,
                             isinstance(self.r, int) and self.r + 1 == NR - 1)

        def walk(eng, emit, peeled=1):
            emit(0, 0, 0, True, False)
            with eng.Fori(0, (NR - 1 - peeled) // 2) as j:
                emit(2 * j + 1, j, 1, False, False)
                emit(2 * j + 2, j + 1, 0, False, False)
            for r in range(NR - peeled, NR):
                emit(r, r // 2, r % 2, False, r == NR - 1)

        one = ExitStack()
        with one:
            G = sb(one, "G", [128, RING, 4 * C])
            ST = sb(one, "ST", [128, 3, CT, PX])
            wconv = sb(one, "wconv", [128, CT, TAPS, C])
            woff = sb(one, "woff", [128, CT, TAPS, 64], F32R)
            xo = sb(one, "xo", [128, 2, CT, 10, W])
            xf = sb(one, "xf", [128, 2, CT, 10, W])
            po = sb(one, "po", [128, 2, 2, CT, 10, W + 2], F32R)
            pf = sb(one, "pf", [128, 2, 2, CT, 10, W + 2], F32R)
            yT = sb(one, "yT", [128, PT, C])
            om_c = sb(one, "om_c", [64, PX])
            om = sb(one, "om", [128, PT, 27])
            base_s = sb(one, "base_s", [128, NR, PT * 18])
            pos = sb(one, "pos", [128, 3, PT * 18])
            posi = sb(one, "posi", [128, PT * 18], I32)
            mk = sb(one, "mk", [128, 3, PT * TAPS])
            quad = sb(one, "quad", [128, NR, NG], I32)
            wts = sb(one, "wts", [128, NR, 4 * NG])
            quad_c = sb(one, "quad_c", [128, 2, NG], I32)
            wts_c = sb(one, "wts_c", [128, 2, 4 * NG])
            xres = sb(one, "xres", [128, 2, CT, PX])
            x1c = sb(one, "x1c", [128, CT, PX])
            h1c = sb(one, "h1c", [128, CT, PX])
            idn = sb(one, "idn", [128, 128])
            gavg = sb(one, "gavg", [128, 128])
            selhl = sb(one, "selhl", [64, 27])
            boff = sb(one, "boff", [64, 1])
            ones = sb(one, "ones", [128, 128])
            xz = sb(one, "xz", [128, 2, CT, PX])
            st0 = sb(one, "st0", [128, CT, NR, 6])
            st1 = sb(one, "st1", [128, CT, NR, 6])
            mv = sb(one, "mv", [128, CT, 2])
            gm = sb(one, "gm", [128, CT, 2])
            gsq = sb(one, "gsq", [128, CT])
            sc0 = sb(one, "sc0", [128, CT])
            bi0 = sb(one, "bi0", [128, CT])
            sc1 = sb(one, "sc1", [128, CT])
            bi1 = sb(one, "bi1", [128, CT])
            wst = sb(one, "wst", [128, 4])
            wmm = sb(one, "wmm", [2, 4])
            wall = sb(one, "wall", [128, 8])

            psA = ps(one, "psA", [128, 512])
            psX = ps(one, "psX", [128, 512])
            psT = ps(one, "psT", [128, CT, PX])
            psD = ps(one, "psD", [128, CT, PX])
            psF = ps(one, "psF", [128, CT, PX])
            ps_yT, ps_om = psX[:, 0:C], psX[:, 256:256 + PT * 27]
            ps_gn0 = psX[:, 384:384 + 2 * CT]
            ps_gn1 = psF[:, 0, 0:2 * CT]
            ps_w_row, ps_w = psD[0:2, 0, 0:128], psD[:, 1, 0:8]
            stage = G[:, 0:5, :].rearrange("p s c -> p (s c)")[:, 0:NW]
            tmpq = G[:, 5:10, :].rearrange("p s c -> p (s c)")[:, 0:NW]
            raw_off = ST[:, 0, :, :].rearrange("p t x -> p (t x)")[:, 0:CT * TAPS * 27].rearrange(
                "p (t k j) -> p t k j", t=CT, k=TAPS)
            zero_sb = xf[:, 0, :, :, :].rearrange("p t h w -> p (t h w)")[:, 0:2 * C]

            s_const, s_zero, s_edge, s_wraw = sem("const_loaded"), sem("zeros_set"), sem("edges_written"), sem("wraw_loaded")
            s_wconv = sem("wconv_loaded")
            z_load = [sem(f"z_x_loaded{i}") for i in range(2)]
            z_stat = sem("z_stats_done")
            s_init = sem("init_steps")
            s_tern, s_wtr, s_wrd, s_wbc = sem("ternary_done"), sem("w_transposed"), sem("w_reduced"), sem("w_broadcast")
            s_woff = sem("woff_split")
            s_gnst, s_gnmm, s_gnv, s_gnsq, s_gnok = sem("gn_moments"), sem("gn_group_sums"), sem("gn_var"), sem("gn_sqrt"), sem("gn_ready")
            s_gch, s_gsum = sem("gn_step"), sem("gn_aggregated")
            CREDIT = 2
            o_load = [sem(f"o_x_loaded{i}") for i in range(2)]
            o_y, o_hi, o_split, o_conv = sem("o_y_ready"), sem("o_hi_ready"), sem("o_split_ready"), sem("o_conv_done")
            o_tr, o_yt, o_tw = sem("o_y_transposed"), sem("o_yT_ready"), sem("o_table_written")
            o_omc, o_om, o_sig, o_ix, o_idx = sem("o_om_evacuated"), sem("o_om_turned"), sem("o_om_ready"), sem("o_index_step"), sem("o_index_ready")
            d_pick, d_qpick = sem("d_weights_picked"), sem("d_rows_picked")
            d_g = [sem(f"d_gathered{i}") for i in range(RING)]
            d_m0, d_mac, d_tr, d_st, d_conv = sem("d_first_corner"), sem("d_mac_done"), sem("d_transposed"), sem("d_st_ready"), sem("d_conv_done")
            d_xl = [sem(f"d_xres_loaded{i}") for i in range(2)]
            d_x1, d_stat, d_store = sem("d_x1_ready"), sem("d_stats_done"), sem("d_x1_stored")
            f_load = [sem(f"f_x1_loaded{i}") for i in range(2)]
            f_y, f_hi, f_split, f_conv = sem("f_y_ready"), sem("f_hi_ready"), sem("f_split_ready"), sem("f_conv_done")
            f_h, f_stat, f_store = sem("f_h1_ready"), sem("f_stats_done"), sem("f_h1_stored")

            def schedule(eng, emit, ahead=False):
                for s in range(-2, NB + 1):
                    def at(r, rh, p, first, last):
                        now = [Chunk(b, r, rh, p, first, last) if 0 <= b < NB else None for b in (s + 2, s + 1, s, s - 1)]
                        if not ahead:
                            return emit(s, *now)
                        if last:
                            then = (Chunk(s + 2, 0, 0, 0, True, False) if 0 <= s + 2 < NB else None, None)
                        else:
                            then = (now[1] and now[1].after(), now[3] and now[3].after())
                        emit(s, *now, *then)
                    walk(eng, at, 3 if ahead else 1)

            O_TAPS = {0: [0, 1], 1: [2, 3], 2: [4, 5], 3: [6, 7], 4: [8]}
            F_TAPS = {0: [0], 1: [1], 2: [2], 3: [3], 4: [4], 5: [5], 6: [6], 7: [7, 8]}
            F_TAPS_FIRST = {3: [0, 1], 4: [2, 3], 5: [4, 5], 6: [6], 7: [7, 8]}
            NORMS = [(0, 0), (0, 1), (0, 2), (1, 0), (0, 3), (1, 1), (1, 2), (1, 3)]
            IXS = 13

            block = one.enter_context(nc.Block())

            @block.sync
            def _(sp):
                for dst, src in ((idn[:], ident), (gavg[:], group_avg), (selhl[:], sel_hl),
                                 (base_s[:].rearrange("p r i -> p (r i)"), base.rearrange("p r i -> p (r i)")),
                                 (raw_off, w_off.rearrange("(t c) k j -> c t k j", c=128)),
                                 (gb[:], bn_params)):
                    sp.dma_start(dst, src).then_inc(s_const, 16)
                sp.wait_ge(s_zero, 2)
                sp.dma_start(boff[0:27, :], b_off.rearrange("(a o) -> a o", o=1)).then_inc(s_const, 16)
                sp.sem_inc(f_store, CREDIT)
                sp.wait_ge(z_stat, CREDIT)

                def load_z(z):
                    hold(sp, z_stat, z.n - 1 + CREDIT)
                    sp.dma_start(xz[:, z.p], rows_of(x, z.b, z.r * RC, RC)).then_inc(z_load[z.p], 16)

                def one_time_loads():
                    sp.dma_start(stage, w1.rearrange("(t c) k o -> c t (k o)", c=128)).then_inc(s_wraw, 16)
                    sp.dma_start(wconv[:].rearrange("p t k o -> p t (k o)"),
                                 w_conv.rearrange("(t c) k o -> c t (k o)", c=128)).then_inc(s_wconv, 16)
                    table_border()

                def table_border():
                    sp.wait_ge(s_zero, 6)
                    rows = [tbl[b][y, :, 2 * q:2 * q + 2, :].rearrange("x q c -> x (q c)") for b in range(NB) for y, q in ((0, 0), (QP - 1, 1))]
                    cols = [tbl[b][:, xx, q, :] for b in range(NB) for xx, q in ((0, 0), (0, 2), (QP - 1, 1), (QP - 1, 3))]
                    for d in rows:
                        sp.dma_start(d, zero_sb[0:QP, 0:d.shape[1]]).then_inc(s_edge, 16)
                    sp.wait_ge(s_edge, 16 * len(rows))
                    for d in cols:
                        sp.dma_start(d, zero_sb[0:QP, 0:d.shape[1]]).then_inc(s_edge, 16)
                def store_x1(b, r, n):
                    hold(sp, d_x1, n + 1 + CREDIT)
                    sp.dma_start(rows_of(x1_d, b, r * RC, RC), x1c[:]).then_inc(d_store, 16)

                def load_f(f):
                    hold(sp, f_split, f.n - 1 + CREDIT)
                    sp.dma_start(flat(xf[:, f.p, :, f.top:f.top + f.rows, :]),
                                 rows_of(x1_d, f.b, f.y0, f.rows)).then_inc(f_load[f.p], 16)

                def load_o(o):
                    hold(sp, o_split, o.n - 1 + CREDIT)
                    hold(sp, o_tr, PT * (o.n - 1) + CREDIT)
                    sp.dma_start(flat(xo[:, o.p, :, o.top:o.top + o.rows, :]),
                                 rows_of(x, o.b, o.y0, o.rows)).then_inc(o_load[o.p], 16)

                def emit(s, z, o, d, f, o2, f2):
                    if d:
                        hold(sp, d_x1, d.n - 1 + CREDIT)
                        sp.dma_start(xres[:, d.p], rows_of(x, d.b, d.r * RC, RC)).then_inc(d_xl[d.p], 16)
                    if z:
                        load_z(z)
                    if s == -1 and o.first:
                        one_time_loads()
                    if d and not d.first:
                        store_x1(d.b, d.r - 1, d.n - 1)
                    if f and f.first:
                        if s == 1:
                            sp.wait_ge(s_edge, 16 * 6 * NB)
                        store_x1(s - 1, NR - 1, f.n + NR - 1)
                        hold(sp, d_store, 16 * (f.n + NR))
                        load_f(f)
                        if s == NB:
                            sp.dma_start(stage, w2.rearrange("(t c) k o -> c t (k o)", c=128)).then_inc(s_wraw, 16)
                    if f2:
                        load_f(f2)
                    if o2:
                        load_o(o2)
                    if o:
                        hold(sp, o_yt, PT * (o.n + 1))
                        for h in range(2):
                            for dy in range(2):
                                for dx in range(2):
                                    dst = tbl[o.b][ds(o.r * RC + h + 1 - dy, PT, step=2), 1 - dx:1 - dx + W, 2 * dy + dx, :]
                                    sp.dma_start(dst.rearrange("t x c -> x t c"),
                                                 yT[64 * h:64 * h + 64, :, :]).then_inc(o_tw, 16)
                    if f:
                        hold(sp, f_h, f.n + 1 + CREDIT)
                        sp.dma_start(rows_of(h1_d, f.b, f.r * RC, RC), h1c[:]).then_inc(f_store, 16)
                schedule(sp, emit, ahead=True)
                hold(sp, f_store, 16 * NCH + CREDIT)
                hold(sp, d_store, 16 * NCH)

            @block.gpsimd
            def _(pool):
                pool.memset(ones[:], 1.0).then_inc(s_zero, 1)
                pool.memset(boff[:], 0.0).then_inc(s_zero, 1)
                pool.memset(xf[:], 0.0).then_inc(s_zero, 1)
                pool.memset(po[:].bitcast(F32), 0.0).then_inc(s_zero, 1)
                pool.memset(pf[:].bitcast(F32), 0.0).then_inc(s_zero, 1)
                pool.memset(eps_t[:], EPS).then_inc(s_zero, 1)

                def emit(s, z, o, d, f):
                    if not d:
                        return
                    if d.first:
                        if s == 0:
                            pool.wait_ge(s_tern, 1)
                            pool.wait_ge(s_edge, 16 * 6 * NB)
                        hold(pool, o_tw, 128 * (d.n + NR))
                    hold(pool, o_idx, d.n + 1)
                    hold(pool, d_tr, TAPS * (d.n - 1) + CREDIT)
                    pool.tensor_copy(quad_c[:, d.p, :], quad[:, ds(d.r, 1), :].rearrange("p r i -> p (r i)")).then_inc(d_qpick, 1)
                    hold(pool, d_qpick, d.n + 1)
                    for i in range(NG):
                        if i % PT == RING % PT:
                            hold(pool, d_tr, TAPS * d.n + (i - RING) // PT + 1 + CREDIT)
                        pool.indirect_dma_start(
                            out=G[:, i % RING, :], out_offset=None, in_=tbl[d.b].rearrange("y x q c -> (y x) (q c)"),
                            in_offset=bass.IndirectOffsetOnAxis(ap=quad_c[:, d.p, i:i + 1], axis=0)).then_inc(d_g[i % RING], 16)
                schedule(pool, emit)

            @block.scalar
            def _(act):
                act.wait_ge(s_zero, 6)
                act.wait_ge(s_woff, 1)
                act.wait_ge(s_const, 112)

                def group_sqrt(norm):
                    act.wait_ge(s_gnv, NORMS.index(norm) + 1)
                    act.activation(gsq[:], gsq[:], ACT.Sqrt, bias=eps_t[:, 0:1]).then_inc(s_gnsq, 1)

                def om_evac(o):
                    act.wait_ge(o_conv, o.n + 1 + CREDIT)
                    act.activation(om_c[:], psA[0:64, :], ACT.Identity, bias=boff[:, 0:1], scale=1.0).then_inc(o_omc, 1)

                def om_turned(o):
                    act.wait_ge(o_om, o.n + 1)
                    need(act, o_idx, o.n)
                    act.activation(om[:].rearrange("p t j -> p (t j)"), ps_om, ACT.Copy).then_inc(o_sig, 1)
                    act.activation(mk[:, 0, :].rearrange("p (t k) -> p t k", t=PT),
                                   ps_om.rearrange("p (t j) -> p t j", t=PT)[:, :, 18:27], ACT.Sigmoid).then_inc(o_sig, 1)

                def normalise(c, src, load, scale, bias, ready, norm):
                    hold(act, load[c.p], 16 * (c.half + 1))
                    if c.first:
                        act.wait_ge(s_gnok, NORMS.index(norm) + 1)
                    for t in range(CT):
                        v = src[:, c.p, t, c.top:c.top + c.rows, :]
                        i = act.activation(v, v, ACT.Identity, bias=bias[:, t:t + 1], scale=scale[:, t:t + 1])
                    i.then_inc(ready, 1)

                def emit(s, z, o, d, f, o2, f2):
                    for k in range(TAPS):
                        if f and f.first and k == 1:
                            group_sqrt((1, f.b))
                        if z and z.last and k == 6:
                            group_sqrt((0, z.b))
                        if d:
                            if k == 0:
                                act.wait_ge(d_pick, d.n + 1)
                            for t in range(PT):
                                i = PT * k + t
                                act.wait_ge(d_g[i % RING], 16 * (NG // RING * d.n + i // RING + 1))
                                g = G[:, i % RING, 0:C]
                                act.activation(g, g, ACT.Copy, scale=wts_c[:, d.p, i:i + 1]).then_inc(d_m0, 1)
                            if k > 0:
                                st_evac(d, k - 1)
                        if o and 2 <= k < 2 + PT:
                            act.wait_ge(o_tr, PT * o.n + k - 1 + CREDIT)
                            if k == 2:
                                need(act, o_tw, 128 * o.n)
                            act.activation(yT[:, k - 2, :], ps_yT, ACT.Copy).then_inc(o_yt, 1)
                        if f and f.first and k == 1:
                            normalise(f, xf, f_load, sc1, bi1, f_y, (1, f.b))
                        if f2 and k == 4:
                            normalise(f2, xf, f_load, sc1, bi1, f_y, None)
                        if o2 and not o2.first and k == 5:
                            normalise(o2, xo, o_load, sc0, bi0, o_y, None)
                        if o and k == 5:
                            om_evac(o)
                        if o and k == 7:
                            om_turned(o)
                        if o2 and o2.first and k == 7:
                            normalise(o2, xo, o_load, sc0, bi0, o_y, (0, o2.b))
                        if f and k == 8:
                            act.wait_ge(f_conv, f.n + 1 + CREDIT)
                            act.wait_ge(f_store, 16 * f.n + CREDIT)
                            act.wait_ge(f_stat, f.n + CREDIT)
                            act.activation(h1c[:], psF[:], ACT.Copy).then_inc(f_h, 1)
                    if d:
                        st_evac(d, TAPS - 1)

                def st_evac(d, k):
                    need(act, d_tr, TAPS * d.n + k + 1 + CREDIT)
                    need(act, d_conv, TAPS * d.n + k - 2)
                    act.activation(ST[:, k % 3], psT[:], ACT.Copy).then_inc(d_st, 1)

                for free in (f_h, d_m0):
                    act.sem_inc(free, CREDIT)
                schedule(act, emit, ahead=True)

            @block.vector
            def _(dve):
                count = [0]

                def step(ins):
                    ins.then_inc(s_init, 1)
                    count[0] += 1
                    dve.wait_ge(s_init, count[0])

                for free in (f_split, o_split, d_x1, d_mac, z_stat, f_stat):
                    dve.sem_inc(free, CREDIT)
                dve.wait_ge(s_const, 112)
                dve.wait_ge(s_zero, 6)
                step(dve.memset(woff[:].bitcast(F32), 0.0))
                step(dve.tensor_copy(woff[:, :, :, 0:27], raw_off))
                for t in range(CT):
                    i = dve.tensor_tensor(woff[:, t, :, 32:59], raw_off[:, t], woff[:, t, :, 0:27].bitcast(F32), ALU.subtract)
                i.then_inc(s_woff, 1)

                def ternary_limits(m, raw):
                    dve.wait_ge(s_wraw, 16 * (m + 1))
                    dve.tensor_reduce(wst[:, 0:1], raw, AX.X, ALU.add)
                    dve.tensor_reduce(wst[:, 1:2], raw, AX.X, ALU.max)
                    step(dve.tensor_reduce(wst[:, 2:3], raw, AX.X, ALU.min))
                    dve.tensor_scalar(wst[:, 2:3], wst[:, 2:3], -1.0, None, ALU.mult).then_inc(s_wtr, 1)
                    dve.wait_ge(s_wrd, 2 * m + 1)
                    step(dve.tensor_reduce(wmm[:, 0:1], ps_w_row, AX.X, ALU.max))
                    dve.tensor_scalar(wmm[:, 1:3], idn[0:2, 0:2], wmm[:, 0:1], None, ALU.mult).then_inc(s_wtr, 1)
                    dve.wait_ge(s_wrd, 2 * m + 2)
                    step(dve.tensor_copy(wall[:, 0:3], ps_w[:, 0:3]))
                    step(dve.tensor_scalar(wall[:, 3:4], wall[:, 0:1], 1.0 / (C * C * TAPS), None, ALU.mult))
                    step(dve.tensor_tensor(wall[:, 1:2], wall[:, 1:2], wall[:, 3:4], ALU.subtract))
                    step(dve.scalar_tensor_tensor(wall[:, 2:3], wall[:, 2:3], -1.0, wall[:, 3:4], ALU.mult, ALU.subtract))
                    step(dve.tensor_tensor(wall[:, 4:5], wall[:, 1:2], wall[:, 2:3], ALU.subtract))
                    step(dve.tensor_scalar(wall[:, 4:5], wall[:, 4:5], 1.0 / 3.0, None, ALU.mult))
                    step(dve.tensor_tensor(wall[:, 5:6], wall[:, 2:3], wall[:, 4:5], ALU.add))
                    step(dve.tensor_tensor(wall[:, 6:7], wall[:, 1:2], wall[:, 4:5], ALU.subtract))

                def ternary_compare(raw):
                    step(dve.tensor_scalar(tmpq, raw, wall[:, 3:4], wall[:, 6:7], ALU.subtract, ALU.is_gt))
                    step(dve.tensor_scalar(raw, raw, wall[:, 3:4], wall[:, 5:6], ALU.subtract, ALU.is_lt))

                def ternary_out():
                    dve.tensor_tensor(qw[:].rearrange("p t k o -> p (t k o)"), tmpq, stage, ALU.subtract).then_inc(s_tern, 1)

                GS = 5

                def norm_moments(norm, stats):
                    c = NORMS.index(norm)
                    for t in range(CT):
                        ins = dve.bn_aggr(mv[:, t, :], stats[:, t].rearrange("p r s -> p (r s)"))
                    ins.then_inc(s_gsum, 1)
                    dve.wait_ge(s_gsum, c + 1)
                    mean, var = mv[:, :, 0], mv[:, :, 1]
                    dve.tensor_tensor(gsq[:], mean, mean, ALU.mult).then_inc(s_gch, 1)
                    dve.wait_ge(s_gch, GS * c + 1)
                    dve.tensor_tensor(var, var, gsq[:], ALU.add).then_inc(s_gnst, 1)

                def norm_variance(norm):
                    c = NORMS.index(norm)
                    dve.wait_ge(s_gnmm, c + 1)
                    dve.tensor_copy(gm[:].rearrange("p k m -> p (k m)"), ps_gn1 if norm[0] else ps_gn0).then_inc(s_gch, 1)
                    dve.wait_ge(s_gch, GS * c + 2)
                    dve.tensor_tensor(gsq[:], gm[:, :, 0], gm[:, :, 0], ALU.mult).then_inc(s_gch, 1)
                    dve.wait_ge(s_gch, GS * c + 3)
                    dve.tensor_tensor(gsq[:], gm[:, :, 1], gsq[:], ALU.subtract).then_inc(s_gch, 1)
                    dve.wait_ge(s_gch, GS * c + 4)
                    dve.tensor_scalar(gsq[:], gsq[:], 0.0, None, ALU.max).then_inc(s_gnv, 1)

                def norm_scale(norm, scale, bias):
                    c = NORMS.index(norm)
                    dve.wait_ge(s_gnsq, c + 1)
                    dve.reciprocal(scale, gsq[:]).then_inc(s_gch, 1)
                    dve.wait_ge(s_gch, GS * c + 5)
                    dve.scalar_tensor_tensor(bias, gm[:, :, 0], -1.0, scale, ALU.mult, ALU.mult).then_inc(s_gnok, 1)

                def split(c, src, pad, y, hi, done, conv):
                    dve.wait_ge(y, c.n + 1)
                    dve.wait_ge(conv, c.n - 1 + CREDIT)
                    rows = slice(c.top, c.top + c.rows)
                    for t in range(CT):
                        i = dve.tensor_copy(pad[:, c.p, 0, t, rows, 1:W + 1], src[:, c.p, t, rows, :])
                    i.then_inc(hi, 1)
                    if c.first or c.last:
                        edge = 0 if c.first else 9
                        for part in range(2):
                            dve.memset(pad[:, c.p, part, :, edge, 1:W + 1].bitcast(F32), 0.0)
                    dve.wait_ge(hi, c.n + 1)
                    for t in range(CT):
                        i = dve.tensor_tensor(pad[:, c.p, 1, t, rows, 1:W + 1], src[:, c.p, t, rows, :],
                                              pad[:, c.p, 0, t, rows, 1:W + 1].bitcast(F32), ALU.subtract)
                    i.then_inc(done, 1)

                def finish_deform(b, r, n, p, half):
                    dve.wait_ge(d_conv, TAPS * (n + 1))
                    dve.wait_ge(d_xl[p], 16 * (half + 1))
                    need(dve, d_store, 16 * n)
                    dve.tensor_tensor(x1c[:], psD[:], xres[:, p], ALU.add).then_inc(d_x1, 1)
                    need(dve, d_x1, n + 1 + CREDIT)
                    for t in range(CT):
                        i = dve.bn_stats(st1[:, t, ds(r, 1), :].rearrange("p r s -> p (r s)"), x1c[:, t, :])
                    i.then_inc(d_stat, 1)

                def take_stats(z):
                    dve.wait_ge(z_load[z.p], 16 * (z.half + 1))
                    for t in range(CT):
                        i = dve.bn_stats(st0[:, t, ds(z.r, 1), :].rearrange("p r s -> p (r s)"), xz[:, z.p, t, :])
                    i.then_inc(z_stat, 1)

                def indices(o):
                    c0 = [IXS * o.n]

                    def go(ins):
                        ins.then_inc(o_ix, 1)
                        c0[0] = c0[0] + 1
                        dve.wait_ge(o_ix, c0[0])
                    P, Fl, Lf = (pos[:, i, :] for i in range(3))
                    v3 = lambda a: a.rearrange("p (t i) -> p t i", t=PT)
                    yx = lambda a, m: a.rearrange("p (t k m) -> p k t m", t=PT, m=2)[:, :, :, m]
                    kt = lambda a: a.rearrange("p (k t) -> p k t", t=PT)
                    w4 = wts[:, ds(o.r, 1), :].rearrange("p r (q i) -> p (r q) i", q=4)
                    dve.wait_ge(o_sig, 2 * (o.n + 1))
                    go(dve.tensor_tensor(v3(P), om[:, :, 0:18], v3(base_s[:, ds(o.r, 1), :].rearrange("p r i -> p (r i)")), ALU.add))
                    go(dve.tensor_scalar(P, P, 0.0, float(H + 1), ALU.max, ALU.min))
                    go(dve.tensor_copy(posi[:], P))
                    go(dve.tensor_copy(Fl, posi[:]))
                    go(dve.tensor_tensor(Lf, Fl, P, ALU.is_gt))
                    go(dve.tensor_tensor(Fl, Fl, Lf, ALU.subtract))
                    go(dve.tensor_scalar(Fl, Fl, float(H), None, ALU.min))
                    go(dve.tensor_tensor(Lf, P, Fl, ALU.subtract))
                    go(dve.tensor_scalar(P, Lf, -1.0, 1.0, ALU.mult, ALU.add))
                    m9 = mk[:, 0, :].rearrange("p (t k) -> p k t", t=PT)
                    go(dve.tensor_tensor(kt(mk[:, 1, :]), m9, yx(P, 0), ALU.mult))
                    go(dve.tensor_tensor(kt(mk[:, 2, :]), m9, yx(Lf, 0), ALU.mult))
                    for q in range(4):
                        ins = dve.tensor_tensor(kt(w4[:, q, :]), kt(mk[:, 1 + q // 2, :]), yx((P, Lf)[q % 2], 1), ALU.mult)
                    go(ins)
                    go(dve.scalar_tensor_tensor(kt(mk[:, 1, :]), yx(Fl, 0), float(QP), yx(Fl, 1), ALU.mult, ALU.add))
                    if not (isinstance(o.b, int) and o.b == 0):
                        dve.wait_ge(d_qpick, o.n - NR + 1)
                    dve.tensor_copy(quad[:, ds(o.r, 1), :].rearrange("p r i -> p (r i)"), mk[:, 1, :]).then_inc(o_idx, 1)

                def emit(s, z, o, d, f, o2, f2):
                    if d:
                        need(dve, d_mac, 3 * NG * (d.n - 1) + CREDIT)
                        need(dve, d_m0, NG * (d.n - 1) + CREDIT)
                        dve.tensor_copy(wts_c[:, d.p, :], wts[:, ds(d.r, 1), :].rearrange("p r i -> p (r i)")).then_inc(d_pick, 1)
                        dve.wait_ge(d_pick, d.n + 1)
                    for k in range(TAPS):
                        if d:
                            for q in range(1, 4):
                                for t in range(PT):
                                    i = PT * k + t
                                    g = G[:, i % RING, :]
                                    if q == 1:
                                        dve.wait_ge(d_m0, NG * d.n + i + 1 + CREDIT)
                                    else:
                                        dve.wait_ge(d_mac, 3 * NG * d.n + 3 * PT * k + PT * (q - 2) + t + 1 + CREDIT)
                                    dve.scalar_tensor_tensor(g[:, 0:C], g[:, q * C:(q + 1) * C], wts_c[:, d.p, q * NG + i:q * NG + i + 1],
                                                             g[:, 0:C], ALU.mult, ALU.add).then_inc(d_mac, 1)
                            if k == 0 and not d.first:
                                finish_deform(d.b, d.r - 1, d.n - 1, 1 - d.p, d.half if d.p else d.half - 1)
                        if k == 0 and f and f.first:
                            finish_deform(s - 1, NR - 1, f.n + NR - 1, 1, f.half + NR // 2 - 1)
                            dve.wait_ge(d_stat, NR * s)
                            norm_moments((1, s - 1), st1)
                            norm_variance((1, s - 1))
                            norm_scale((1, s - 1), sc1[:], bi1[:])
                        if f and f.first and k == 1:
                            split(f, xf, pf, f_y, f_hi, f_split, f_conv)
                        if z and k == 2:
                            take_stats(z)
                        if z and z.last and k == 3:
                            dve.wait_ge(z_stat, NR * (s + 3) + CREDIT)
                            norm_moments((0, z.b), st0)
                        if z and z.last and k == 4:
                            norm_variance((0, z.b))
                        if z and z.last and k == 6:
                            norm_scale((0, z.b), sc0[:], bi0[:])
                        if f2 and k == 4:
                            split(f2, xf, pf, f_y, f_hi, f_split, f_conv)
                        if o2 and k == (7 if o2.first else 6):
                            split(o2, xo, po, o_y, o_hi, o_split, o_conv)
                        if o and k == 8:
                            indices(o)
                    if f:
                        dve.wait_ge(f_h, f.n + 1 + CREDIT)
                        for t in range(CT):
                            ins = dve.bn_stats(bn1_stats[:, t, ds(f.n, 1), :].rearrange("p r s -> p (r s)"), h1c[:, t, :])
                        ins.then_inc(f_stat, 1)
                    if s == -1 and o.first:
                        ternary_limits(0, stage)
                    if s == -1 and o.last:
                        ternary_compare(stage)
                        ternary_out()
                    if s == NB and f.first:
                        ternary_limits(1, stage)
                        ternary_compare(stage)
                schedule(dve, emit, ahead=True)
                dve.wait_ge(f_conv, NCH + CREDIT)
                ternary_out()

            @block.tensor
            def _(pe):
                pe.wait_ge(s_zero, 6)
                pe.wait_ge(s_const, 112)

                def weight_extremes(m):
                    pe.wait_ge(s_wtr, 2 * m + 1)
                    pe.transpose(ps_w_row, wst[:, 1:3], idn[:]).then_inc(s_wrd, 1)
                    pe.wait_ge(s_wtr, 2 * m + 2)
                    pe.matmul(ps_w[:, 0:1], ones[:], wst[:, 0:1], start=True, stop=True)
                    pe.matmul(ps_w[:, 1:3], ones[0:2, :], wmm[:, 1:3], start=True, stop=True).then_inc(s_wrd, 1)

                def group_sums(norm):
                    pe.wait_ge(s_gnst, NORMS.index(norm) + 1)
                    pe.matmul(ps_gn1 if norm[0] else ps_gn0, gavg[:], mv[:].rearrange("p k m -> p (k m)"),
                              start=True, stop=True).then_inc(s_gnmm, 1)

                def conv_tap(c, pad, w, acc, tap, first, last, m):
                    dy, dx = tap // 3, tap % 3
                    for oc in range(acc.shape[1]):
                        for t in range(CT):
                            for part in range(2):
                                ins = pe.matmul(acc[:, oc, :].rearrange("p (h w) -> p h w", h=RC), w[:, t, tap, oc * m:(oc + 1) * m],
                                                pad[:, c.p, part, t, dy:dy + RC, dx:dx + W],
                                                start=(first and t == 0 and part == 0), stop=(last and t == CT - 1 and part == 1))
                    return ins

                def deform_tap(d, k):
                    pe.wait_ge(d_st, TAPS * d.n + k + 1)
                    if k == 0:
                        need(pe, d_x1, d.n + CREDIT)
                    for oc in range(CT):
                        for t in range(CT):
                            ins = pe.matmul(psD[:, oc, :], wconv[:, t, k, oc * 128:(oc + 1) * 128], ST[:, k % 3, t, :],
                                            start=(k == 0 and t == 0), stop=(k == TAPS - 1 and t == CT - 1))
                    ins.then_inc(d_conv, 1)

                def turn_om(o):
                    pe.wait_ge(o_omc, o.n + 1)
                    for t in range(PT):
                        ins = pe.matmul(ps_om[:, t * 27:(t + 1) * 27], om_c[:, t * 128:(t + 1) * 128], selhl[:], start=True, stop=True)
                    ins.then_inc(o_om, 1)

                def emit(s, z, o, d, f):
                    if s == -1 and o.first:
                        pe.wait_ge(s_woff, 1)
                    if s == 0 and d.first:
                        pe.wait_ge(s_wconv, 16)
                    for k in range(TAPS):
                        if f and f.first and k == 1:
                            need(pe, f_h, f.n + CREDIT)
                            group_sums((1, f.b))
                        if z and z.last and k == 5:
                            if o:
                                pe.wait_ge(o_yt, PT * (o.n + 1))
                            group_sums((0, z.b))
                        if d:
                            need(pe, d_mac, 3 * NG * d.n + 3 * PT * (k + 1) + CREDIT)
                            need(pe, d_st, TAPS * d.n + k)
                            for t in range(PT):
                                for c in range(CT):
                                    ins = pe.transpose(psT[:, c, t * 128:(t + 1) * 128],
                                                       G[:, (PT * k + t) % RING, c * 128:(c + 1) * 128], idn[:])
                            ins.then_inc(d_tr, 1)
                            if k > 0:
                                deform_tap(d, k - 1)
                        if o:
                            for tap in O_TAPS.get(k, []):
                                if tap == 0:
                                    pe.wait_ge(o_split, o.n + 1 + CREDIT)
                                    need(pe, o_omc, o.n)
                                ins = conv_tap(o, po, woff, psA[0:64, :].rearrange("p (o x) -> p o x", o=1), tap, tap == 0, tap == TAPS - 1, 64)
                                if tap == TAPS - 1:
                                    ins.then_inc(o_conv, 1)
                            if k == 6:
                                pe.wait_ge(o_yt, PT * (o.n + 1))
                                if z and z.last:
                                    pe.wait_ge(s_gnv, NORMS.index((0, z.b)) + 1)
                                turn_om(o)
                            if k == 1:
                                need(pe, o_sig, 2 * o.n)
                            if 1 <= k < 1 + PT:
                                need(pe, o_yt, PT * o.n + k - 1)
                                for c in range(CT):
                                    ins = pe.transpose(ps_yT[:, c * 128:(c + 1) * 128],
                                                       xo[:, o.p, c, 1 + 2 * (k - 1):3 + 2 * (k - 1), :].rearrange("p h w -> p (h w)"), idn[:])
                                ins.then_inc(o_tr, 1)
                        if f:
                            for tap in (F_TAPS_FIRST if f.first else F_TAPS).get(k, []):
                                if tap == 0:
                                    if s == 1 and f.first:
                                        pe.wait_ge(s_tern, 1)
                                    pe.wait_ge(f_split, f.n + 1 + CREDIT)
                                    pe.wait_ge(f_h, f.n + CREDIT)
                                ins = conv_tap(f, pf, qw, psF, tap, tap == 0, tap == TAPS - 1, 128)
                                if tap == TAPS - 1:
                                    ins.then_inc(f_conv, 1)
                    if d:
                        deform_tap(d, TAPS - 1)
                    if s == -1 and o.first:
                        weight_extremes(0)
                    if s == NB and f.first:
                        weight_extremes(1)
                for free in (f_conv, o_conv, o_tr, d_tr):
                    pe.sem_inc(free, CREDIT)
                schedule(pe, emit)

        two = ExitStack()
        names2 = ExitStack()
        with two, names2:
            def sem2(n):
                return names2.enter_context(nc.semaphore(n))

            h2 = sb(two, "h2", [128, CT, NCH * PX])
            work = sb(two, "work", [128, 6, CT * PX])
            pg = sb(two, "pg", [128, 2, 2, CT, 10, W + 2], F32R)
            flat_work = work[:].rearrange("p s x -> p (s x)")
            XN = 2 * CT * 10 * W
            xg = flat_work[:, 0:XN].rearrange("p (q t h w) -> p q t h w", q=2, t=CT, h=10)
            bn2_stats = sb(two, "bn2_stats", [128, CT, NCH, 6])
            mv2 = sb(two, "mv2", [128, CT, 2])
            sq = sb(two, "sq", [128, CT])
            scale_b = sb(two, "scale_b", [128, 2, CT])
            bias_b = sb(two, "bias_b", [128, 2, CT])
            psG = ps(two, "psG", [128, 2, CT, PX])

            g_zero, g_ag, g_sq, g_bn, g_bch = (sem2(n) for n in ("borders_zero", "bn_moments", "bn_sqrt", "bn_ready", "bn_step"))
            g_load = [sem2(f"g_h1_loaded{i}") for i in range(2)]
            g_y, g_hi, g_split, g_conv, g_h, g_stat = (sem2(n) for n in ("g_y", "g_hi", "g_split", "g_conv", "g_h2", "g_stats"))
            e_lx = [sem2(f"e_x1_loaded{i}") for i in range(2)]
            e_lh = [sem2(f"e_h1_loaded{i}") for i in range(4)]
            e_st = [sem2(f"e_out_stored{i}") for i in range(4)]
            e_r1, e_mac, e_r2, e_sum = (sem2(n) for n in ("e_relu1", "e_mixed", "e_relu2", "e_out_ready"))
            CR = 2

            def batches(eng, emit):
                with eng.Fori(0, NB) as b:
                    walk(eng, lambda r, rh, p, first, last: emit(Chunk(b, r, rh, p, first, last)))

            block2 = two.enter_context(nc.Block())

            @block2.sync
            def _(sp):
                def emit(c):
                    hold(sp, g_split, c.n - 1 + CR)
                    sp.dma_start(flat(xg[:, c.p, :, c.top:c.top + c.rows, :]), rows_of(h1_d, c.b, c.y0, c.rows)).then_inc(g_load[c.p], 16)
                batches(sp, emit)
                hold(sp, g_conv, NCH + CR)

                def load_four(j):
                    for u in range(4):
                        b, r = j // 2, 4 * (j % 2) + u
                        hold(sp, e_st[u], 16 * j)
                        sp.dma_start(work[:, u, :].rearrange("p (t x) -> p t x", t=CT), rows_of(h1_d, b, r * RC, RC)).then_inc(e_lh[u], 16)
                        hold(sp, e_sum, 4 * j + u - 1 + CR)
                        sp.dma_start(work[:, 4 + u % 2, :].rearrange("p (t x) -> p t x", t=CT), rows_of(x1_d, b, r * RC, RC)).then_inc(e_lx[u % 2], 16)
                load_four(0)
                with sp.Fori(1, NCH // 4) as j:
                    load_four(j)

            @block2.gpsimd
            def _(pool):
                pool.memset(pg[:].bitcast(F32), 0.0).then_inc(g_zero, 1)

                def emit(c):
                    hold(pool, g_hi, c.n + 1)
                    rows = slice(c.top, c.top + c.rows)
                    if c.first or c.last:
                        edge = 0 if c.first else 9
                        for t in range(CT):
                            pool.memset(pg[:, c.p, 1, t, edge, 1:W + 1].bitcast(F32), 0.0)
                            pool.memset(pg[:, c.p, 0, t, edge, 1:W + 1].bitcast(F32), 0.0)
                    for t in range(CT):
                        i = pool.tensor_tensor(pg[:, c.p, 1, t, rows, 1:W + 1], xg[:, c.p, t, rows, :],
                                               pg[:, c.p, 0, t, rows, 1:W + 1].bitcast(F32), ALU.subtract)
                    i.then_inc(g_split, 1)
                pool.sem_inc(g_split, CR)
                batches(pool, emit)
                with pool.Fori(0, NCH // 4) as j:
                    for u in range(4):
                        hold(pool, e_sum, 4 * j + u + 1 + CR)
                        pool.dma_start(rows_of(out, j // 2, (4 * (j % 2) + u) * RC, RC),
                                       work[:, u, :].rearrange("p (t x) -> p t x", t=CT)).then_inc(e_st[u], 16)
                for u in range(4):
                    hold(pool, e_st[u], 16 * (NCH // 4))

            @block2.scalar
            def _(act):
                act.wait_ge(g_ag, 1)
                act.activation(sq[:], sq[:], ACT.Sqrt, bias=eps_t[:, 0:1]).then_inc(g_sq, 1)
                act.wait_ge(g_bn, 1)
                act.wait_ge(g_zero, 1)

                def emit(c):
                    act.wait_ge(g_load[c.p], 16 * (c.half + 1))
                    act.wait_ge(g_conv, c.n - 1 + CR)
                    rows = slice(c.top, c.top + c.rows)
                    for t in range(CT):
                        act.activation(pg[:, c.p, 0, t, rows, 1:W + 1], xg[:, c.p, t, rows, :], ACT.Relu,
                                       bias=bias_b[:, 0, t:t + 1], scale=scale_b[:, 0, t:t + 1])
                    for t in range(CT):
                        i = act.activation(xg[:, c.p, t, rows, :], xg[:, c.p, t, rows, :], ACT.Relu,
                                           bias=bias_b[:, 0, t:t + 1], scale=scale_b[:, 0, t:t + 1])
                    i.then_inc(g_hi, 1)
                batches(act, emit)
                act.wait_ge(g_ag, 2)
                act.activation(sq[:], sq[:], ACT.Sqrt, bias=eps_t[:, 0:1]).then_inc(g_sq, 1)
                act.wait_ge(g_bn, 2)
                with act.Fori(0, NCH // 4) as j:
                    def relu1(u):
                        act.wait_ge(e_lh[u], 16 * (j + 1))
                        for t in range(CT):
                            v = work[:, u, t * PX:(t + 1) * PX]
                            i = act.activation(v, v, ACT.Relu, bias=bias_b[:, 0, t:t + 1], scale=scale_b[:, 0, t:t + 1])
                        i.then_inc(e_r1, 1)

                    def relu2(u):
                        act.wait_ge(e_mac, 4 * j + u + 1)
                        for t in range(CT):
                            v = work[:, u, t * PX:(t + 1) * PX]
                            i = act.activation(v, v, ACT.Relu, bias=bias_b[:, 1, t:t + 1], scale=1.0)
                        i.then_inc(e_r2, 1)
                    relu1(0)
                    for u in range(1, 4):
                        relu1(u)
                        relu2(u - 1)
                    relu2(3)

            @block2.vector
            def _(dve):
                def batch_norm(m, stats):
                    for t in range(CT):
                        i = dve.bn_aggr(mv2[:, t, :], stats[:, t].rearrange("p n s -> p (n s)"))
                    i.then_inc(g_bch, 1)
                    dve.wait_ge(g_bch, 4 * m + 1)
                    dve.tensor_copy(sq[:], mv2[:, :, 1]).then_inc(g_ag, 1)
                    dve.wait_ge(g_sq, m + 1)
                    dve.reciprocal(sq[:], sq[:]).then_inc(g_bch, 1)
                    dve.wait_ge(g_bch, 4 * m + 2)
                    dve.tensor_tensor(scale_b[:, m, :], sq[:], gb[:, 2 * m, :], ALU.mult).then_inc(g_bch, 1)
                    dve.wait_ge(g_bch, 4 * m + 3)
                    dve.tensor_tensor(bias_b[:, m, :], mv2[:, :, 0], scale_b[:, m, :], ALU.mult).then_inc(g_bch, 1)
                    dve.wait_ge(g_bch, 4 * m + 4)
                    dve.tensor_tensor(bias_b[:, m, :], gb[:, 2 * m + 1, :], bias_b[:, m, :], ALU.subtract).then_inc(g_bn, 1)

                batch_norm(0, bn1_stats)

                def emit(c):
                    dve.wait_ge(g_conv, c.n + 1 + CR)
                    dst = h2[:, :, ds(c.n * PX, PX)]
                    dve.tensor_copy(dst, psG[:, c.p]).then_inc(g_h, 1)
                    for t in range(CT):
                        i = dve.bn_stats(bn2_stats[:, t, ds(c.n, 1), :].rearrange("p r s -> p (r s)"), psG[:, c.p, t, :])
                    i.then_inc(g_stat, 1)
                dve.sem_inc(g_stat, CR)
                dve.sem_inc(e_sum, CR)
                batches(dve, emit)
                dve.wait_ge(g_stat, NCH + CR)
                dve.wait_ge(g_h, NCH)
                batch_norm(1, bn2_stats)
                with dve.Fori(0, NCH // 4) as j:
                    def mix(u):
                        dve.wait_ge(e_r1, 4 * j + u + 1)
                        for t in range(CT):
                            v = work[:, u, t * PX:(t + 1) * PX]
                            i = dve.scalar_tensor_tensor(v, h2[:, t, ds((4 * j + u) * PX, PX)], scale_b[:, 1, t:t + 1], v, ALU.mult, ALU.add)
                        i.then_inc(e_mac, 1)

                    def add_x1(u):
                        dve.wait_ge(e_r2, 4 * j + u + 1)
                        dve.wait_ge(e_lx[u % 2], 32 * j + 16 * (u // 2) + 16)
                        dve.tensor_tensor(work[:, u, :], work[:, u, :], work[:, 4 + u % 2, :], ALU.add).then_inc(e_sum, 1)
                    mix(0)
                    for u in range(1, 4):
                        mix(u)
                        add_x1(u - 1)
                    add_x1(3)

            @block2.tensor
            def _(pe):
                def emit(c):
                    pe.wait_ge(g_split, c.n + 1 + CR)
                    pe.wait_ge(g_stat, c.n - 1 + CR)
                    for tap in range(TAPS):
                        dy, dx = tap // 3, tap % 3
                        for oc in range(CT):
                            for t in range(CT):
                                for part in range(2):
                                    i = pe.matmul(psG[:, c.p, oc, :].rearrange("p (h w) -> p h w", h=RC), qw[:, t, tap, oc * 128:(oc + 1) * 128],
                                                  pg[:, c.p, part, t, dy:dy + RC, dx:dx + W],
                                                  start=(tap == 0 and t == 0 and part == 0),
                                                  stop=(tap == TAPS - 1 and t == CT - 1 and part == 1))
                    i.then_inc(g_conv, 1)
                pe.sem_inc(g_conv, CR)
                batches(pe, emit)


def kernel(x, L0_conv_w_off, L0_conv_b_off, L0_conv_w_conv, L1_conv_w1, L1_conv_gamma1, L1_conv_beta1,
           L1_conv_w2, L1_conv_gamma2, L1_conv_beta2):
    import numpy as np
    import concourse.bacc as bacc
    from concourse import mybir
    from concourse.bass_utils import run_bass_kernel_spmd as run

    def by_input(w):
        w = np.asarray(w)
        return np.ascontiguousarray(w.reshape(w.shape[0], w.shape[1], 9).transpose(1, 2, 0))

    eye = np.eye(128, dtype=np.float32)
    group = np.kron(np.eye(16, dtype=np.float32), np.full((8, 8), 1 / 8, np.float32))
    sel = np.zeros((64, 27), np.float32)
    sel[np.arange(27), np.arange(27)] = 1
    sel[32 + np.arange(27), np.arange(27)] = 1
    p, r, t, k = np.ix_(np.arange(128), np.arange(8), np.arange(4), np.arange(9))
    grid = np.stack([8 * r + 2 * t + p // 64 + k // 3, p % 64 + k % 3 + 0 * (r + t)], axis=-1)
    grid = np.ascontiguousarray(grid.reshape(128, 8, 72).astype(np.float32))

    params = np.stack([np.asarray(v) for v in (L1_conv_gamma1, L1_conv_beta1, L1_conv_gamma2, L1_conv_beta2)])
    params = np.ascontiguousarray(params.reshape(4, 2, 128).transpose(2, 0, 1))

    ins = {"x": np.asarray(x), "w_off": by_input(L0_conv_w_off), "b_off": np.asarray(L0_conv_b_off),
           "w_conv": by_input(L0_conv_w_conv), "w1": by_input(L1_conv_w1), "w2": by_input(L1_conv_w2),
           "bn_params": params, "ident": eye, "group_avg": group, "sel_hl": sel, "base": grid}
    nc = bacc.Bacc("TRN2", target_bir_lowering=False, num_devices=1)
    args = [nc.dram_tensor(f"in_{n}", a.shape, mybir.dt.from_np(a.dtype), kind="ExternalInput").ap() for n, a in ins.items()]
    args.append(nc.dram_tensor("out", (4, 256, 64, 64), mybir.dt.float32, kind="ExternalOutput").ap())
    build(nc, *args)
    r = run(nc, [{f"in_{n}": a for n, a in ins.items()}], core_ids=[0])
    return r.results[0]["out"]
```

```python
def build(nc, x, w_off, b_off, w_conv, w1, w2, bn_params, ident, group_avg, sel_hl, base, out):
    import concourse.bass as bass
    from concourse import mybir
    from contextlib import ExitStack

    F32, F32R, I32 = mybir.dt.float32, mybir.dt.float32r, mybir.dt.int32
    ALU, ACT, AX = mybir.AluOpType, mybir.ActivationFunctionType, mybir.AxisListType
    ds = bass.ds

    NB, C, H, W = 4, 256, 64, 64
    CT = C // 128
    TAPS = 9
    RC = 8
    PX = RC * W
    NR = H // RC
    NCH = NB * NR
    PT = PX // 128
    NG = TAPS * PT
    RING = 12
    PAIR_ROWS, XP = H + 1, W + 2
    NW = CT * TAPS * C
    EPS = 1e-5

    tbl = [nc.dram_tensor(f"pixel_pairs{b}", (PAIR_ROWS, XP, 2, C), F32).ap() for b in range(NB)]
    x1_d = nc.dram_tensor("x1", (NB, C, H, W), F32).ap()
    h1_d = nc.dram_tensor("h1", (NB, C, H, W), F32).ap()

    def rows_of(t, b, r0, n):
        v = t.rearrange("b (t c) h w -> b c t h w", c=128)
        return v[ds(b, 1), :, :, ds(r0, n), :].rearrange("b c t h w -> (b c) t (h w)")

    def flat(ap):
        return ap.rearrange("p t h w -> p t (h w)")

    outer = ExitStack()
    names = ExitStack()

    def sem(n):
        return names.enter_context(nc.semaphore(n))

    def need(eng, s, v):
        if not isinstance(v, int) or v > 0:
            eng.wait_ge(s, v)

    s_held = sem("held")

    def hold(eng, s, v):
        if isinstance(v, int) and v <= 0:
            return
        eng.wait_ge(s, v)
        eng.sem_inc(s_held, 1)

    def sb(stack, n, shape, dt=F32):
        return stack.enter_context(nc.sbuf_tensor(n, shape, dt))

    def ps(stack, n, shape, dt=F32):
        return stack.enter_context(nc.psum_tensor(n, shape, dt))

    with outer, names:
        qw = sb(outer, "qw", [128, CT, TAPS, C], F32R)
        bn1_stats = sb(outer, "bn1_stats", [128, CT, NCH, 6])
        po = sb(outer, "po", [128, 2, 2, CT, 10, W + 2], F32R)
        po_flat = po[:].rearrange("p q s t h w -> p (q s t h w)")
        wino2 = po_flat[:, 0:CT * 3 * C].rearrange("p (t k o) -> p t k o", t=CT, k=3)
        gb = sb(outer, "gb", [128, 4, CT])
        eps_t = sb(outer, "eps_t", [128, 1])

        class Chunk:
            def __init__(self, b, r, r_half, p, first, last):
                self.b, self.r, self.p, self.first, self.last = b, r, p, first, last
                self.n, self.half = b * NR + r, b * (NR // 2) + r_half
                self.top = 1 if first else 0
                self.rows = 10 - (1 if first else 0) - (1 if last else 0)
                self.y0 = r * RC - (0 if first else 1)

            def is_row(self, r):
                return isinstance(self.r, int) and self.r == r

            def after(self):
                return Chunk(self.b, self.r + 1, self.half - self.b * (NR // 2) + self.p, 1 - self.p, False,
                             isinstance(self.r, int) and self.r + 1 == NR - 1)

        def walk(eng, emit, peeled):
            emit(0, 0, 0, True, False)
            with eng.Fori(0, (NR - 1 - peeled) // 2) as j:
                emit(2 * j + 1, j, 1, False, False)
                emit(2 * j + 2, j + 1, 0, False, False)
            for r in range(NR - peeled, NR):
                emit(r, r // 2, r % 2, False, r == NR - 1)

        one = ExitStack()
        with one:
            G = sb(one, "G", [128, RING, 4 * C])
            ST = sb(one, "ST", [128, 3, CT, PX])
            wconv = sb(one, "wconv", [128, CT, TAPS, C])
            woff = sb(one, "woff", [128, CT, TAPS, 64], F32R)
            xo = sb(one, "xo", [128, 2, CT, 10, W])
            xf = sb(one, "xf", [128, 2, CT, 10, W])
            pf = sb(one, "pf", [128, 2, 2, CT, 10, W + 2], F32R)
            yT = sb(one, "yT", [128, PT, C])
            om_c = sb(one, "om_c", [64, PX])
            om = sb(one, "om", [128, PT, 27])
            base_s = sb(one, "base_s", [128, NR, PT * 18])
            pos = sb(one, "pos", [128, 3, PT * 18])
            posi = sb(one, "posi", [128, PT * 18], I32)
            mk = sb(one, "mk", [128, 3, PT * TAPS])
            quad = sb(one, "quad", [128, NR, NG], I32)
            wts = sb(one, "wts", [128, NR, 4 * NG])
            quad_c = sb(one, "quad_c", [128, 2, NG], I32)
            wts_c = sb(one, "wts_c", [128, 2, 4 * NG])
            xres = sb(one, "xres", [128, 2, CT, PX])
            x1c = sb(one, "x1c", [128, CT, PX])
            h1c = sb(one, "h1c", [128, CT, PX])
            idn = sb(one, "idn", [128, 128])
            gavg = sb(one, "gavg", [128, 128])
            selhl = sb(one, "selhl", [64, 27])
            boff = sb(one, "boff", [64, 1])
            ones = sb(one, "ones", [128, 128])
            xz = sb(one, "xz", [128, 2, CT, PX])
            st0 = sb(one, "st0", [128, CT, NR, 6])
            st1 = sb(one, "st1", [128, CT, NR, 6])
            mv = sb(one, "mv", [128, CT, 2])
            gm = sb(one, "gm", [128, CT, 2])
            gsq = sb(one, "gsq", [128, CT])
            sc0 = sb(one, "sc0", [128, CT])
            bi0 = sb(one, "bi0", [128, CT])
            sc1 = sb(one, "sc1", [128, CT])
            bi1 = sb(one, "bi1", [128, CT])
            wst = sb(one, "wst", [128, 3, 2])
            wmm = sb(one, "wmm", [2, 4])
            wall = sb(one, "wall", [128, 8])

            psA = ps(one, "psA", [128, 512])
            psX = ps(one, "psX", [128, 512])
            psT = ps(one, "psT", [128, CT, PX])
            psD = ps(one, "psD", [128, CT, PX])
            psF = ps(one, "psF", [128, CT, PX])
            ps_yT, ps_om = psX[:, 0:C], psX[:, 256:256 + PT * 27]
            ps_gn0 = psX[:, 384:384 + 2 * CT]
            ps_gn1 = psF[:, 0, 0:2 * CT]
            ps_w_row = [psF[0:2, 0, 0:128], psD[0:2, 0, 0:128]]
            ps_w = [psF[:, 1, 0:3], psD[:, 1, 0:3]]
            HW, STAGE1 = NW // CT, 7
            stage1 = G[:, STAGE1:, :].rearrange("p s c -> p (s c)")[:, 0:NW].rearrange("p (t i) -> p t i", t=CT)
            stage2 = G[:, 0:5, :].rearrange("p s c -> p (s c)")[:, 0:NW]
            above2 = G[:, 5:10, :].rearrange("p s c -> p (s c)")[:, 0:NW]
            raw_off = ST[:, 0, :, :].rearrange("p t x -> p (t x)")[:, 0:CT * TAPS * 27].rearrange(
                "p (t k j) -> p t k j", t=CT, k=TAPS)
            zero_sb = xf[:, 0, :, :, :].rearrange("p t h w -> p (t h w)")[:, 0:2 * C]

            s_const, s_zero, s_edge, s_wraw = sem("const_loaded"), sem("zeros_set"), sem("edges_written"), sem("wraw_loaded")
            s_wconv = sem("wconv_loaded")
            z_load = [sem(f"z_x_loaded{i}") for i in range(2)]
            z_stat = sem("z_stats_done")
            s_init = sem("init_steps")
            s_tern, s_wtr, s_wrd = sem("ternary_done"), sem("w_sums_step"), sem("w_sums_turned")
            s_woff = sem("woff_split")
            s_gnst, s_gnmm, s_gnv, s_gnsq, s_gnok = sem("gn_moments"), sem("gn_group_sums"), sem("gn_var"), sem("gn_sqrt"), sem("gn_ready")
            s_gch, s_gsum = sem("gn_step"), sem("gn_aggregated")
            CREDIT = 2
            o_load = [sem(f"o_x_loaded{i}") for i in range(2)]
            o_y, o_hi, o_split, o_conv = sem("o_y_ready"), sem("o_hi_ready"), sem("o_split_ready"), sem("o_conv_done")
            o_tr, o_yt, o_tw = sem("o_y_transposed"), sem("o_yT_ready"), sem("o_table_written")
            o_omc, o_om, o_sig, o_ix, o_idx = sem("o_om_evacuated"), sem("o_om_turned"), sem("o_om_ready"), sem("o_index_step"), sem("o_index_ready")
            d_pick, d_qpick = sem("d_weights_picked"), sem("d_rows_picked")
            d_g = [sem(f"d_gathered{i}") for i in range(RING)]
            d_m0, d_mac, d_tr, d_st, d_conv = sem("d_first_corner"), sem("d_mac_done"), sem("d_transposed"), sem("d_st_ready"), sem("d_conv_done")
            d_xl = [sem(f"d_xres_loaded{i}") for i in range(2)]
            d_x1, d_stat, d_store = sem("d_x1_ready"), sem("d_stats_done"), sem("d_x1_stored")
            f_load = [sem(f"f_x1_loaded{i}") for i in range(2)]
            f_y, f_hi, f_split, f_conv = sem("f_y_ready"), sem("f_hi_ready"), sem("f_split_ready"), sem("f_conv_done")
            f_h, f_stat, f_store = sem("f_h1_ready"), sem("f_stats_done"), sem("f_h1_stored")

            def schedule(eng, emit):
                for s in range(-2, NB + 1):
                    def at(r, rh, p, first, last):
                        now = [Chunk(b, r, rh, p, first, last) if 0 <= b < NB else None for b in (s + 2, s + 1, s, s - 1)]
                        if last:
                            then = (Chunk(s + 2, 0, 0, 0, True, False) if 0 <= s + 2 < NB else None, None)
                        else:
                            then = (now[1] and now[1].after(), now[3] and now[3].after())
                        emit(s, *now, *then)
                    walk(eng, at, 3)

            O_TAPS = {0: [0, 1, 2], 1: [3, 4], 2: [5, 6], 3: [7, 8]}
            F_TAPS = {0: [0], 1: [1], 2: [2], 3: [3], 4: [4], 5: [5], 6: [6], 7: [7, 8]}
            F_TAPS_FIRST = {3: [0], 4: [1, 2], 5: [3, 4], 6: [5, 6], 7: [7, 8]}
            def o_step(d, o2):
                return (7 if o2.first else 6) if d or o2.first else 1

            def pixel_major(d, o):
                return yT if d or not o.p else G[:, 0, :].rearrange("p (t c) -> p t c", t=PT)

            def f_norm(d):
                return 3 if d else 1

            def f_step(d, f):
                return (4 if f.first else 3) if d else 1

            NORMS = [(0, 0), (0, 1), (0, 2), (1, 0), (0, 3), (1, 1), (1, 2), (1, 3)]
            TW = 4 * 16
            IXS, IX0 = 13, 9

            block = one.enter_context(nc.Block())

            @block.sync
            def _(sp):
                for dst, src in ((idn[:], ident), (gavg[:], group_avg), (selhl[:], sel_hl),
                                 (base_s[:].rearrange("p r i -> p (r i)"), base.rearrange("p r i -> p (r i)")),
                                 (raw_off, w_off.rearrange("(t c) k j -> c t k j", c=128)),
                                 (gb[:], bn_params)):
                    sp.dma_start(dst, src).then_inc(s_const, 16)
                sp.wait_ge(s_zero, 2)
                sp.dma_start(boff[0:27, :], b_off.rearrange("(a o) -> a o", o=1)).then_inc(s_const, 16)
                sp.sem_inc(f_store, CREDIT)
                sp.sem_inc(o_tw, CREDIT)
                sp.wait_ge(z_stat, CREDIT)

                def load_z(z):
                    hold(sp, z_stat, z.n - 1 + CREDIT)
                    sp.dma_start(xz[:, z.p], rows_of(x, z.b, z.r * RC, RC)).then_inc(z_load[z.p], 16)

                def one_time_loads():
                    sp.dma_start(wconv[:].rearrange("p t k o -> p t (k o)"),
                                 w_conv.rearrange("(t c) k o -> c t (k o)", c=128)).then_inc(s_wconv, 16)
                    table_border()

                def table_border():
                    sp.wait_ge(s_zero, 6)
                    for b in range(NB):
                        for y, q in ((0, 0), (H, 1)):
                            sp.dma_start(tbl[b][y, 1:W + 1, q, :], zero_sb[0:W, 0:C]).then_inc(s_edge, 16)
                        for xx in (0, W + 1):
                            sp.dma_start(tbl[b][:, xx].rearrange("y q c -> y (q c)"), zero_sb[0:PAIR_ROWS, 0:2 * C]).then_inc(s_edge, 16)

                def store_x1(b, r, n):
                    hold(sp, d_x1, n + 1 + CREDIT)
                    sp.dma_start(rows_of(x1_d, b, r * RC, RC), x1c[:]).then_inc(d_store, 16)

                def load_f(f):
                    hold(sp, f_split, f.n - 1 + CREDIT)
                    sp.dma_start(flat(xf[:, f.p, :, f.top:f.top + f.rows, :]),
                                 rows_of(x1_d, f.b, f.y0, f.rows)).then_inc(f_load[f.p], 16)

                def load_o(o):
                    hold(sp, o_split, o.n - 1 + CREDIT)
                    hold(sp, o_tr, PT * (o.n - 1) + CREDIT)
                    sp.dma_start(flat(xo[:, o.p, :, o.top:o.top + o.rows, :]),
                                 rows_of(x, o.b, o.y0, o.rows)).then_inc(o_load[o.p], 16)

                def emit(s, z, o, d, f, o2, f2):
                    if d:
                        hold(sp, d_x1, d.n - 1 + CREDIT)
                        sp.dma_start(xres[:, d.p], rows_of(x, d.b, d.r * RC, RC)).then_inc(d_xl[d.p], 16)
                    if z:
                        load_z(z)
                    if d and not d.first:
                        store_x1(d.b, d.r - 1, d.n - 1)
                    if f and f.first:
                        if s == 1:
                            sp.wait_ge(s_edge, 16 * 4 * NB)
                        hold(sp, d_store, 16 * (f.n + NR - 1))
                        load_f(f)
                        store_x1(s - 1, NR - 1, f.n + NR - 1)
                        hold(sp, d_store, 16 * (f.n + NR))
                        if s == NB:
                            sp.dma_start(stage2, w2.rearrange("(t c) k o -> c t (k o)", c=128)).then_inc(s_wraw, 16)
                    if f2:
                        load_f(f2)
                    if o2:
                        load_o(o2)
                    if s == -1 and o.first:
                        sp.dma_start(stage1, w1.rearrange("(t c) k o -> c t (k o)", c=128)).then_inc(s_wraw, 16)
                    if s == -1 and o.is_row(5):
                        one_time_loads()
                    if o:
                        hold(sp, o_yt, PT * (o.n + 1))
                        for h in range(2):
                            for up in range(2):
                                dst = tbl[o.b][ds(o.r * RC + h + 1 - up, PT, step=2), 1:1 + W, up, :]
                                sp.dma_start(dst.rearrange("t x c -> x t c"),
                                             pixel_major(d, o)[64 * h:64 * h + 64, :, :]).then_inc(o_tw, 16)
                    if f:
                        hold(sp, f_h, f.n + 1 + CREDIT)
                        sp.dma_start(rows_of(h1_d, f.b, f.r * RC, RC), h1c[:]).then_inc(f_store, 16)
                schedule(sp, emit)
                hold(sp, f_store, 16 * NCH + CREDIT)
                hold(sp, d_store, 16 * NCH)

            @block.gpsimd
            def _(pool):
                pool.memset(ones[:], 1.0).then_inc(s_zero, 1)
                pool.memset(boff[:], 0.0).then_inc(s_zero, 1)
                pool.memset(xf[:], 0.0).then_inc(s_zero, 1)
                pool.memset(po[:].bitcast(F32), 0.0).then_inc(s_zero, 1)
                pool.memset(pf[:].bitcast(F32), 0.0).then_inc(s_zero, 1)
                pool.memset(eps_t[:], EPS).then_inc(s_zero, 1)

                def emit(s, z, o, d, f, o2, f2):
                    if not d:
                        return
                    if d.first:
                        if s == 0:
                            pool.wait_ge(s_edge, 16 * 4 * NB)
                        hold(pool, o_tw, TW * (d.n + NR) + CREDIT)
                    hold(pool, o_idx, d.n + 1)
                    hold(pool, d_tr, TAPS * (d.n - 1) + CREDIT)
                    pool.tensor_copy(quad_c[:, d.p, :], quad[:, ds(d.r, 1), :].rearrange("p r i -> p (r i)")).then_inc(d_qpick, 1)
                    hold(pool, d_qpick, d.n + 1)
                    for i in range(NG):
                        if s == 0 and d.first and i == STAGE1:
                            hold(pool, s_tern, 1)
                        if i % PT == RING % PT:
                            hold(pool, d_tr, TAPS * d.n + (i - RING) // PT + 1 + CREDIT)
                        pool.indirect_dma_start(
                            out=G[:, i % RING, :], out_offset=None, in_=tbl[d.b].rearrange("y x q c -> (y x) (q c)"),
                            in_offset=bass.IndirectOffsetOnAxis(ap=quad_c[:, d.p, i:i + 1], axis=0)).then_inc(d_g[i % RING], 16)
                schedule(pool, emit)

            @block.scalar
            def _(act):
                act.wait_ge(s_zero, 6)
                act.wait_ge(s_woff, 1)
                act.wait_ge(s_const, 112)

                def group_sqrt(norm):
                    act.wait_ge(s_gnv, NORMS.index(norm) + 1)
                    act.activation(gsq[:], gsq[:], ACT.Sqrt, bias=eps_t[:, 0:1]).then_inc(s_gnsq, 1)

                def om_evac(o):
                    act.wait_ge(o_conv, o.n + 1 + CREDIT)
                    act.activation(om_c[:], psA[0:64, :], ACT.Identity, bias=boff[:, 0:1], scale=1.0).then_inc(o_omc, 1)

                def om_turned(o):
                    act.wait_ge(o_om, o.n + 1)
                    need(act, o_idx, o.n)
                    act.activation(om[:].rearrange("p t j -> p (t j)"), ps_om, ACT.Copy).then_inc(o_sig, 1)
                    act.activation(mk[:, 0, :].rearrange("p (t k) -> p t k", t=PT),
                                   ps_om.rearrange("p (t j) -> p t j", t=PT)[:, :, 18:27], ACT.Sigmoid).then_inc(o_sig, 1)

                def normalise(c, src, load, scale, bias, ready, norm):
                    hold(act, load[c.p], 16 * (c.half + 1))
                    if c.first:
                        act.wait_ge(s_gnok, NORMS.index(norm) + 1)
                    for t in range(CT):
                        v = src[:, c.p, t, c.top:c.top + c.rows, :]
                        i = act.activation(v, v, ACT.Identity, bias=bias[:, t:t + 1], scale=scale[:, t:t + 1])
                    i.then_inc(ready, 1)

                def emit(s, z, o, d, f, o2, f2):
                    for k in range(TAPS):
                        if d:
                            if k == 0:
                                act.wait_ge(d_pick, d.n + 1)
                            for t in range(PT):
                                i = PT * k + t
                                act.wait_ge(d_g[i % RING], 16 * (NG // RING * d.n + i // RING + 1))
                                g = G[:, i % RING, 0:C]
                                act.activation(g, g, ACT.Copy, scale=wts_c[:, d.p, i:i + 1]).then_inc(d_m0, 1)
                        if f and f.first and k == (2 if d else 1):
                            group_sqrt((1, f.b))
                        if z and z.last and k == 6:
                            group_sqrt((0, z.b))
                        if d and k > 0:
                            st_evac(d, k - 1)
                        if o and 1 <= k < 1 + PT:
                            act.wait_ge(o_tr, PT * o.n + k + CREDIT)
                            if k == 1:
                                need(act, o_tw, TW * (o.n if d else o.n - 1) + CREDIT)
                            act.activation(pixel_major(d, o)[:, k - 1, :], ps_yT, ACT.Copy).then_inc(o_yt, 1)
                        if f and f.first and k == f_norm(d):
                            normalise(f, xf, f_load, sc1, bi1, f_y, (1, f.b))
                        if f2 and k == f_step(d, f):
                            normalise(f2, xf, f_load, sc1, bi1, f_y, None)
                        if o2 and not o2.first and k == o_step(d, o2) - (1 if d else 0):
                            normalise(o2, xo, o_load, sc0, bi0, o_y, None)
                        if o and k == 4:
                            om_evac(o)
                        if o and k == 6:
                            om_turned(o)
                        if o2 and o2.first and k == 7:
                            normalise(o2, xo, o_load, sc0, bi0, o_y, (0, o2.b))
                        if f and k == 8:
                            act.wait_ge(f_conv, f.n + 1 + CREDIT)
                            act.wait_ge(f_store, 16 * f.n + CREDIT)
                            act.wait_ge(f_stat, f.n + CREDIT)
                            act.activation(h1c[:], psF[:], ACT.Copy).then_inc(f_h, 1)
                    if d:
                        st_evac(d, TAPS - 1)

                def st_evac(d, k):
                    need(act, d_tr, TAPS * d.n + k + 1 + CREDIT)
                    need(act, d_conv, TAPS * d.n + k - 2)
                    act.activation(ST[:, k % 3], psT[:], ACT.Copy).then_inc(d_st, 1)

                for free in (f_h, d_m0):
                    act.sem_inc(free, CREDIT)
                schedule(act, emit)

            @block.vector
            def _(dve):
                count = [0]

                def step(ins):
                    ins.then_inc(s_init, 1)
                    count[0] += 1
                    dve.wait_ge(s_init, count[0])

                for free in (f_split, o_split, d_x1, d_mac, z_stat, f_stat):
                    dve.sem_inc(free, CREDIT)
                dve.wait_ge(s_const, 112)
                step(dve.memset(woff[:].bitcast(F32), 0.0))
                step(dve.tensor_copy(woff[:, :, :, 0:27], raw_off))
                for t in range(CT):
                    i = dve.tensor_tensor(woff[:, t, :, 32:59], raw_off[:, t], woff[:, t, :, 0:27].bitcast(F32), ALU.subtract)
                i.then_inc(s_woff, 1)

                def weight_sums(part, raw):
                    dve.tensor_reduce(wst[:, 0, part:part + 1], raw, AX.X, ALU.add)
                    dve.tensor_reduce(wst[:, 1, part:part + 1], raw, AX.X, ALU.max)
                    return dve.tensor_reduce(wst[:, 2, part:part + 1], raw, AX.X, ALU.min)

                def weight_sums_ready(parts):
                    if parts == 2:
                        dve.tensor_tensor(wst[:, 0, 0:1], wst[:, 0, 0:1], wst[:, 0, 1:2], ALU.add)
                        dve.tensor_tensor(wst[:, 1, 0:1], wst[:, 1, 0:1], wst[:, 1, 1:2], ALU.max)
                        step(dve.tensor_tensor(wst[:, 2, 0:1], wst[:, 2, 0:1], wst[:, 2, 1:2], ALU.min))
                    dve.tensor_scalar(wst[:, 2, 0:1], wst[:, 2, 0:1], -1.0, None, ALU.mult).then_inc(s_wtr, 1)

                def weight_extremes(m):
                    dve.wait_ge(s_wrd, 2 * m + 1)
                    step(dve.tensor_reduce(wmm[:, 0:1], ps_w_row[m], AX.X, ALU.max))
                    dve.tensor_scalar(wmm[:, 1:3], idn[0:2, 0:2], wmm[:, 0:1], None, ALU.mult).then_inc(s_wtr, 1)

                def weight_limits(m):
                    dve.wait_ge(s_wrd, 2 * m + 2)
                    step(dve.tensor_copy(wall[:, 0:3], ps_w[m]))
                    step(dve.tensor_scalar(wall[:, 3:4], wall[:, 0:1], 1.0 / (C * C * TAPS), None, ALU.mult))
                    step(dve.tensor_tensor(wall[:, 1:2], wall[:, 1:2], wall[:, 3:4], ALU.subtract))
                    step(dve.scalar_tensor_tensor(wall[:, 2:3], wall[:, 2:3], -1.0, wall[:, 3:4], ALU.mult, ALU.subtract))
                    step(dve.tensor_tensor(wall[:, 4:5], wall[:, 1:2], wall[:, 2:3], ALU.subtract))
                    step(dve.tensor_scalar(wall[:, 4:5], wall[:, 4:5], 1.0 / 3.0, None, ALU.mult))
                    step(dve.tensor_tensor(wall[:, 5:6], wall[:, 2:3], wall[:, 4:5], ALU.add))
                    step(dve.tensor_tensor(wall[:, 6:7], wall[:, 1:2], wall[:, 4:5], ALU.subtract))

                def compare(above, raw):
                    dve.tensor_scalar(above, raw, wall[:, 3:4], wall[:, 6:7], ALU.subtract, ALU.is_gt)
                    step(dve.tensor_scalar(raw, raw, wall[:, 3:4], wall[:, 5:6], ALU.subtract, ALU.is_lt))

                def winograd_weights():
                    g = [above2.rearrange("p (t y i) -> p t y i", t=CT, y=3)[:, :, y, :] for y in range(3)]
                    both = stage2.rearrange("p (t y i) -> p t y i", t=CT, y=3)[:, :, 0, :]
                    dve.tensor_tensor(both, g[0], g[2], ALU.add)
                    step(dve.tensor_scalar(g[1], g[1], 0.5, None, ALU.mult))
                    dve.scalar_tensor_tensor(wino2.rearrange("p t k o -> p t (k o)"), both, 0.5, g[1], ALU.mult, ALU.subtract)
                    step(dve.scalar_tensor_tensor(g[1], both, 0.5, g[1], ALU.mult, ALU.add))

                def compare_w1(part):
                    q = qw[:, part].rearrange("p k o -> p (k o)")
                    compare(q, stage1[:, part])
                    return dve.tensor_tensor(q, q.bitcast(F32), stage1[:, part], ALU.subtract)

                GS = 5

                def norm_moments(norm, stats):
                    c = NORMS.index(norm)
                    for t in range(CT):
                        ins = dve.bn_aggr(mv[:, t, :], stats[:, t].rearrange("p r s -> p (r s)"))
                    ins.then_inc(s_gsum, 1)
                    dve.wait_ge(s_gsum, c + 1)
                    mean, var = mv[:, :, 0], mv[:, :, 1]
                    dve.tensor_tensor(gsq[:], mean, mean, ALU.mult).then_inc(s_gch, 1)
                    dve.wait_ge(s_gch, GS * c + 1)
                    dve.tensor_tensor(var, var, gsq[:], ALU.add).then_inc(s_gnst, 1)

                def norm_variance(norm):
                    c = NORMS.index(norm)
                    dve.wait_ge(s_gnmm, c + 1)
                    dve.tensor_copy(gm[:].rearrange("p k m -> p (k m)"), ps_gn1 if norm[0] else ps_gn0).then_inc(s_gch, 1)
                    dve.wait_ge(s_gch, GS * c + 2)
                    dve.tensor_tensor(gsq[:], gm[:, :, 0], gm[:, :, 0], ALU.mult).then_inc(s_gch, 1)
                    dve.wait_ge(s_gch, GS * c + 3)
                    dve.tensor_tensor(gsq[:], gm[:, :, 1], gsq[:], ALU.subtract).then_inc(s_gch, 1)
                    dve.wait_ge(s_gch, GS * c + 4)
                    dve.tensor_scalar(gsq[:], gsq[:], 0.0, None, ALU.max).then_inc(s_gnv, 1)

                def norm_scale(norm, scale, bias):
                    c = NORMS.index(norm)
                    dve.wait_ge(s_gnsq, c + 1)
                    dve.reciprocal(scale, gsq[:]).then_inc(s_gch, 1)
                    dve.wait_ge(s_gch, GS * c + 5)
                    dve.scalar_tensor_tensor(bias, gm[:, :, 0], -1.0, scale, ALU.mult, ALU.mult).then_inc(s_gnok, 1)

                def split(c, src, pad, y, hi, done, conv):
                    dve.wait_ge(y, c.n + 1)
                    dve.wait_ge(conv, c.n - 1 + CREDIT)
                    rows = slice(c.top, c.top + c.rows)
                    for t in range(CT):
                        i = dve.tensor_copy(pad[:, c.p, 0, t, rows, 1:W + 1], src[:, c.p, t, rows, :])
                    i.then_inc(hi, 1)
                    if c.first or c.last:
                        edge = 0 if c.first else 9
                        for part in range(2):
                            dve.memset(pad[:, c.p, part, :, edge, 1:W + 1].bitcast(F32), 0.0)
                    dve.wait_ge(hi, c.n + 1)
                    for t in range(CT):
                        i = dve.tensor_tensor(pad[:, c.p, 1, t, rows, 1:W + 1], src[:, c.p, t, rows, :],
                                              pad[:, c.p, 0, t, rows, 1:W + 1].bitcast(F32), ALU.subtract)
                    i.then_inc(done, 1)

                def finish_deform(b, r, n, p, half):
                    dve.wait_ge(d_conv, TAPS * (n + 1))
                    dve.wait_ge(d_xl[p], 16 * (half + 1))
                    need(dve, d_store, 16 * n)
                    dve.tensor_tensor(x1c[:], psD[:], xres[:, p], ALU.add).then_inc(d_x1, 1)
                    need(dve, d_x1, n + 1 + CREDIT)
                    for t in range(CT):
                        i = dve.bn_stats(st1[:, t, ds(r, 1), :].rearrange("p r s -> p (r s)"), x1c[:, t, :])
                    i.then_inc(d_stat, 1)

                def take_stats(z):
                    dve.wait_ge(z_load[z.p], 16 * (z.half + 1))
                    for t in range(CT):
                        i = dve.bn_stats(st0[:, t, ds(z.r, 1), :].rearrange("p r s -> p (r s)"), xz[:, z.p, t, :])
                    i.then_inc(z_stat, 1)

                def indices(o, part):
                    c0 = [IXS * o.n + (IX0 if part else 0)]

                    def go(ins):
                        ins.then_inc(o_ix, 1)
                        c0[0] = c0[0] + 1
                        dve.wait_ge(o_ix, c0[0])
                    P, Fl, Lf = (pos[:, i, :] for i in range(3))
                    v3 = lambda a: a.rearrange("p (t i) -> p t i", t=PT)
                    yx = lambda a, m: a.rearrange("p (t k m) -> p k t m", t=PT, m=2)[:, :, :, m]
                    kt = lambda a: a.rearrange("p (k t) -> p k t", t=PT)
                    if part == 0:
                        dve.wait_ge(o_sig, 2 * (o.n + 1))
                        go(dve.tensor_tensor(v3(P), om[:, :, 0:18], v3(base_s[:, ds(o.r, 1), :].rearrange("p r i -> p (r i)")), ALU.add))
                        go(dve.tensor_scalar(P, P, 0.0, float(H + 1), ALU.max, ALU.min))
                        go(dve.tensor_copy(posi[:], P))
                        go(dve.tensor_copy(Fl, posi[:]))
                        go(dve.tensor_tensor(Lf, Fl, P, ALU.is_gt))
                        go(dve.tensor_tensor(Fl, Fl, Lf, ALU.subtract))
                        go(dve.tensor_scalar(Fl, Fl, float(H), None, ALU.min))
                        go(dve.tensor_tensor(Lf, P, Fl, ALU.subtract))
                        go(dve.tensor_scalar(P, Lf, -1.0, 1.0, ALU.mult, ALU.add))
                        return
                    w4 = wts[:, ds(o.r, 1), :].rearrange("p r (q i) -> p (r q) i", q=4)
                    m9 = mk[:, 0, :].rearrange("p (t k) -> p k t", t=PT)
                    go(dve.tensor_tensor(kt(mk[:, 1, :]), m9, yx(P, 0), ALU.mult))
                    go(dve.tensor_tensor(kt(mk[:, 2, :]), m9, yx(Lf, 0), ALU.mult))
                    for q in range(4):
                        ins = dve.tensor_tensor(kt(w4[:, q, :]), kt(mk[:, 1 + q % 2, :]), yx((P, Lf)[q // 2], 1), ALU.mult)
                    go(ins)
                    go(dve.scalar_tensor_tensor(kt(mk[:, 1, :]), yx(Fl, 0), float(XP), yx(Fl, 1), ALU.mult, ALU.add))
                    if not (isinstance(o.b, int) and o.b == 0):
                        dve.wait_ge(d_qpick, o.n - NR + 1)
                    dve.tensor_copy(quad[:, ds(o.r, 1), :].rearrange("p r i -> p (r i)"), mk[:, 1, :]).then_inc(o_idx, 1)

                def emit(s, z, o, d, f, o2, f2):
                    if d:
                        need(dve, d_mac, 3 * NG * (d.n - 1) + CREDIT)
                        need(dve, d_m0, NG * (d.n - 1) + CREDIT)
                        dve.tensor_copy(wts_c[:, d.p, :], wts[:, ds(d.r, 1), :].rearrange("p r i -> p (r i)")).then_inc(d_pick, 1)
                        dve.wait_ge(d_pick, d.n + 1)
                    if s == NB and f.is_row(5):
                        weight_extremes(1)
                    for k in range(TAPS):
                        if d:
                            for q in range(1, 4):
                                for t in range(PT):
                                    i = PT * k + t
                                    g = G[:, i % RING, :]
                                    if q == 1:
                                        dve.wait_ge(d_m0, NG * d.n + i + 1 + CREDIT)
                                    else:
                                        dve.wait_ge(d_mac, 3 * NG * d.n + 3 * PT * k + PT * (q - 2) + t + 1 + CREDIT)
                                    dve.scalar_tensor_tensor(g[:, 0:C], g[:, q * C:(q + 1) * C], wts_c[:, d.p, q * NG + i:q * NG + i + 1],
                                                             g[:, 0:C], ALU.mult, ALU.add).then_inc(d_mac, 1)
                            if k == 0 and not d.first:
                                finish_deform(d.b, d.r - 1, d.n - 1, 1 - d.p, d.half if d.p else d.half - 1)
                        if k == 0 and f and f.first:
                            finish_deform(s - 1, NR - 1, f.n + NR - 1, 1, f.half + NR // 2 - 1)
                            dve.wait_ge(d_stat, NR * s)
                            norm_moments((1, s - 1), st1)
                        if f and f.first and k == (1 if d else 0):
                            norm_variance((1, s - 1))
                        if f and f.first and k == (2 if d else 0):
                            norm_scale((1, s - 1), sc1[:], bi1[:])
                        if f and f.first and k == f_norm(d):
                            split(f, xf, pf, f_y, f_hi, f_split, f_conv)
                        if z and k == 2:
                            take_stats(z)
                        if s == -1 and k == 5 and o.first:
                            dve.wait_ge(s_wraw, 16)
                            weight_sums(0, stage1[:, 0])
                        if s == -1 and k == 2 and o.is_row(5):
                            step(weight_sums(1, stage1[:, 1]))
                            weight_sums_ready(2)
                        if s == -1 and k == 1 and o.is_row(6):
                            weight_extremes(0)
                        if z and z.last and k == 3:
                            dve.wait_ge(z_stat, NR * (s + 3) + CREDIT)
                            norm_moments((0, z.b), st0)
                        if z and z.last and k == 5:
                            norm_variance((0, z.b))
                        if z and z.last and k == (7 if d else 6):
                            norm_scale((0, z.b), sc0[:], bi0[:])
                        if f2 and k == f_step(d, f):
                            split(f2, xf, pf, f_y, f_hi, f_split, f_conv)
                        if o2 and k == o_step(d, o2):
                            split(o2, xo, po, o_y, o_hi, o_split, o_conv)
                        if o and k in (7, 8):
                            indices(o, k - 7)
                        if s == -1 and k == 4 and o.is_row(6):
                            weight_limits(0)
                            compare_w1(1)
                        if s == -1 and k == 2 and o.last:
                            compare_w1(0).then_inc(s_tern, 1)
                        if s == NB and f.last and k == 8:
                            dve.wait_ge(f_conv, NCH + CREDIT)
                            dve.tensor_copy(qw[:].rearrange("p t k o -> p (t k o)"), above2).then_inc(s_tern, 1)
                        if f and k == 8:
                            dve.wait_ge(f_h, f.n + 1 + CREDIT)
                            for t in range(CT):
                                ins = dve.bn_stats(bn1_stats[:, t, ds(f.n, 1), :].rearrange("p r s -> p (r s)"), h1c[:, t, :])
                            ins.then_inc(f_stat, 1)
                    if s == NB and f.first:
                        dve.wait_ge(s_wraw, 32)
                        step(weight_sums(0, stage2))
                        weight_sums_ready(1)
                    if s == NB and f.is_row(5):
                        weight_limits(1)
                        compare(above2, stage2)
                    if s == NB and f.is_row(6):
                        step(dve.tensor_tensor(above2, above2, stage2, ALU.subtract))
                        winograd_weights()
                schedule(dve, emit)

            @block.tensor
            def _(pe):
                pe.wait_ge(s_zero, 6)
                pe.wait_ge(s_const, 112)

                def turn_extremes(m):
                    pe.wait_ge(s_wtr, 2 * m + 1)
                    pe.transpose(ps_w_row[m], wst[:, 1:3, 0], idn[:]).then_inc(s_wrd, 1)

                def spread_limits(m):
                    pe.wait_ge(s_wtr, 2 * m + 2)
                    pe.matmul(ps_w[m][:, 0:1], ones[:], wst[:, 0, 0:1], start=True, stop=True)
                    pe.matmul(ps_w[m][:, 1:3], ones[0:2, :], wmm[:, 1:3], start=True, stop=True).then_inc(s_wrd, 1)

                def group_sums(norm):
                    pe.wait_ge(s_gnst, NORMS.index(norm) + 1)
                    pe.matmul(ps_gn1 if norm[0] else ps_gn0, gavg[:], mv[:].rearrange("p k m -> p (k m)"),
                              start=True, stop=True).then_inc(s_gnmm, 1)

                def conv_tap(c, pad, w, acc, tap, first, last, m):
                    dy, dx = tap // 3, tap % 3
                    for oc in range(acc.shape[1]):
                        for t in range(CT):
                            for part in range(2):
                                ins = pe.matmul(acc[:, oc, :].rearrange("p (h w) -> p h w", h=RC), w[:, t, tap, oc * m:(oc + 1) * m],
                                                pad[:, c.p, part, t, dy:dy + RC, dx:dx + W],
                                                start=(first and t == 0 and part == 0), stop=(last and t == CT - 1 and part == 1))
                    return ins

                def deform_tap(d, k):
                    pe.wait_ge(d_st, TAPS * d.n + k + 1)
                    if k == 0:
                        need(pe, d_x1, d.n + CREDIT)
                    for oc in range(CT):
                        for t in range(CT):
                            ins = pe.matmul(psD[:, oc, :], wconv[:, t, k, oc * 128:(oc + 1) * 128], ST[:, k % 3, t, :],
                                            start=(k == 0 and t == 0), stop=(k == TAPS - 1 and t == CT - 1))
                    ins.then_inc(d_conv, 1)

                def turn_om(o):
                    pe.wait_ge(o_omc, o.n + 1)
                    for t in range(PT):
                        ins = pe.matmul(ps_om[:, t * 27:(t + 1) * 27], om_c[:, t * 128:(t + 1) * 128], selhl[:], start=True, stop=True)
                    ins.then_inc(o_om, 1)

                def emit(s, z, o, d, f, o2, f2):
                    if s == -1 and o.first:
                        pe.wait_ge(s_woff, 1)
                    if s == 0 and d.first:
                        pe.wait_ge(s_wconv, 16)
                    if s == -1 and o.is_row(6):
                        turn_extremes(0)
                    if s == NB and f.is_row(5):
                        turn_extremes(1)
                    if s == NB and f.is_row(6):
                        spread_limits(1)
                    for k in range(TAPS):
                        if s == -1 and o.is_row(6) and k == 3:
                            spread_limits(0)
                        if f and f.first and k == 1:
                            need(pe, f_h, f.n + CREDIT)
                            group_sums((1, f.b))
                        if z and z.last and k == 5:
                            if o:
                                pe.wait_ge(o_yt, PT * (o.n + 1))
                            group_sums((0, z.b))
                        if d:
                            need(pe, d_mac, 3 * NG * d.n + 3 * PT * (k + 1) + CREDIT)
                            need(pe, d_st, TAPS * d.n + k)
                            for t in range(PT):
                                for c in range(CT):
                                    ins = pe.transpose(psT[:, c, t * 128:(t + 1) * 128],
                                                       G[:, (PT * k + t) % RING, c * 128:(c + 1) * 128], idn[:])
                            ins.then_inc(d_tr, 1)
                            if k > 0:
                                deform_tap(d, k - 1)
                        if o:
                            for tap in O_TAPS.get(k, []):
                                if tap == 0:
                                    pe.wait_ge(o_split, o.n + 1 + CREDIT)
                                    need(pe, o_omc, o.n)
                                ins = conv_tap(o, po, woff, psA[0:64, :].rearrange("p (o x) -> p o x", o=1), tap, tap == 0, tap == TAPS - 1, 64)
                                if tap == TAPS - 1:
                                    ins.then_inc(o_conv, 1)
                            if k == 5:
                                pe.wait_ge(o_yt, PT * (o.n + 1))
                                if z and z.last:
                                    pe.wait_ge(s_gnv, NORMS.index((0, z.b)) + 1)
                                turn_om(o)
                            if k == 0:
                                need(pe, o_sig, 2 * o.n)
                            if k < PT:
                                need(pe, o_yt, PT * o.n + k)
                                for c in range(CT):
                                    ins = pe.transpose(ps_yT[:, c * 128:(c + 1) * 128],
                                                       xo[:, o.p, c, 1 + 2 * k:3 + 2 * k, :].rearrange("p h w -> p (h w)"), idn[:])
                                ins.then_inc(o_tr, 1)
                        if f:
                            for tap in (F_TAPS_FIRST if f.first else F_TAPS).get(k, []):
                                if tap == 0:
                                    if s == 1 and f.first:
                                        pe.wait_ge(s_tern, 1)
                                    pe.wait_ge(f_split, f.n + 1 + CREDIT)
                                    pe.wait_ge(f_h, f.n + CREDIT)
                                ins = conv_tap(f, pf, qw, psF, tap, tap == 0, tap == TAPS - 1, 128)
                                if tap == TAPS - 1:
                                    ins.then_inc(f_conv, 1)
                    if d:
                        deform_tap(d, TAPS - 1)
                for free in (f_conv, o_conv, o_tr, d_tr):
                    pe.sem_inc(free, CREDIT)
                schedule(pe, emit)

        two = ExitStack()
        names2 = ExitStack()
        with two, names2:
            PLANES, RP = 4, RC // 2

            def sem2(n):
                return names2.enter_context(nc.semaphore(n))

            h2 = sb(two, "h2", [128, CT, NCH * PX])
            XN, VN, PN = 2 * CT * 10 * W, CT * PLANES * RP * W, PLANES * RP * (W + 2)
            area = sb(two, "area", [128, XN + VN])
            xg = area[:, 0:XN].rearrange("p (q t h w) -> p q t h w", q=2, t=CT, h=10)
            V = area[:, XN:XN + VN].rearrange("p (t j i w) -> p t j i w", t=CT, j=PLANES, i=RP)
            h1w, x1w = (area[:, i * CT * PX:(i + 2) * CT * PX].rearrange("p (s x) -> p s x", s=2) for i in (0, 2))
            LENT = 3
            lent = po_flat[:, CT * 3 * C:CT * 3 * C + LENT * PN].rearrange("p (n r w) -> p n r w", n=LENT, w=W + 2)
            own = sb(two, "pg", [128, 8 - LENT, PLANES * RP, W + 2], F32R)

            def pg(parity, part, t):
                n = 4 * parity + 2 * part + t
                return lent[:, n] if n < LENT else own[:, n - LENT]
            bn2_stats = bn1_stats
            mv2 = sb(two, "mv2", [128, CT, 2])
            sq = sb(two, "sq", [128, CT])
            scale_b = sb(two, "scale_b", [128, 2, CT])
            bias_b = sb(two, "bias_b", [128, 2, CT])
            psG = ps(two, "psG", [128, 2, CT, PLANES, RP * W])

            g_zero, g_ag, g_sq, g_bn, g_bch = (sem2(n) for n in ("borders_zero", "bn_moments", "bn_sqrt", "bn_ready", "bn_step"))
            g_load = [sem2(f"g_h1_loaded{i}") for i in range(2)]
            g_y, g_edge, g_v, g_hi, g_split, g_conv = (sem2(n) for n in ("g_y", "g_edge_zero", "g_planes", "g_hi", "g_split", "g_conv"))
            g_part, g_h, g_stat = (sem2(n) for n in ("g_h2_begun", "g_h2", "g_stats"))
            e_lx = [sem2(f"e_x1_loaded{i}") for i in range(2)]
            e_lh = [sem2(f"e_h1_loaded{i}") for i in range(2)]
            e_st = sem2("e_out_stored")
            e_r1, e_mac, e_r2, e_sum = (sem2(n) for n in ("e_relu1", "e_mixed", "e_relu2", "e_out_ready"))
            CR = 2

            def batches(eng, emit):
                with eng.Fori(0, NB) as b:
                    walk(eng, lambda r, rh, p, first, last: emit(Chunk(b, r, rh, p, first, last)), 1)

            block2 = two.enter_context(nc.Block())

            @block2.sync
            def _(sp):
                def emit(c):
                    hold(sp, g_v, c.n - 1 + CR)
                    sp.dma_start(flat(xg[:, c.p, :, c.top:c.top + c.rows, :]), rows_of(h1_d, c.b, c.y0, c.rows)).then_inc(g_load[c.p], 16)
                batches(sp, emit)
                hold(sp, g_split, NCH + CR)

                with sp.Fori(0, NCH // NR) as j:
                    for u in range(NR):
                        b, r = j, u
                        hold(sp, e_mac, NR * j + u - 1 + CR)
                        sp.dma_start(h1w[:, u % 2, :].rearrange("p (t x) -> p t x", t=CT), rows_of(h1_d, b, r * RC, RC)).then_inc(e_lh[u % 2], 16)
                        hold(sp, e_sum, NR * j + u - 1 + CR)
                        sp.dma_start(x1w[:, u % 2, :].rearrange("p (t x) -> p t x", t=CT), rows_of(x1_d, b, r * RC, RC)).then_inc(e_lx[u % 2], 16)

            @block2.gpsimd
            def _(pool):
                for side in (0, W + 1):
                    for pieces in (lent, own):
                        ins = pool.memset(pieces[:, :, :, side:side + 1].bitcast(F32), 0.0)
                ins.then_inc(g_zero, 1)

                def emit(c):
                    hold(pool, g_hi, c.n + 1)
                    for t in range(CT):
                        i = pool.tensor_tensor(pg(c.p, 1, t)[:, :, 1:W + 1], V[:, t].rearrange("p j i w -> p (j i) w"),
                                               pg(c.p, 0, t)[:, :, 1:W + 1].bitcast(F32), ALU.subtract)
                    i.then_inc(g_split, 1)
                pool.sem_inc(g_split, CR)
                batches(pool, emit)
                with pool.Fori(0, NCH // NR) as j:
                    for u in range(NR):
                        hold(pool, e_sum, NR * j + u + 1 + CR)
                        pool.dma_start(rows_of(out, j, u * RC, RC),
                                       h2[:, :, ds((NR * j + u) * PX, PX)]).then_inc(e_st, 16)
                hold(pool, e_st, 16 * NCH)

            @block2.scalar
            def _(act):
                act.wait_ge(g_ag, 1)
                act.activation(sq[:], sq[:], ACT.Sqrt, bias=eps_t[:, 0:1]).then_inc(g_sq, 1)
                act.wait_ge(g_bn, 1)
                act.wait_ge(g_zero, 1)

                def emit(c):
                    act.wait_ge(g_load[c.p], 16 * (c.half + 1))
                    rows = slice(c.top, c.top + c.rows)
                    for t in range(CT):
                        i = act.activation(xg[:, c.p, t, rows, :], xg[:, c.p, t, rows, :], ACT.Relu,
                                           bias=bias_b[:, 0, t:t + 1], scale=scale_b[:, 0, t:t + 1])
                    i.then_inc(g_y, 1)
                    act.wait_ge(g_v, c.n + 1 + CR)
                    act.wait_ge(g_conv, c.n - 1 + CR)
                    for t in range(CT):
                        i = act.activation(pg(c.p, 0, t)[:, :, 1:W + 1], V[:, t].rearrange("p j i w -> p (j i) w"), ACT.Copy)
                    i.then_inc(g_hi, 1)
                batches(act, emit)
                act.wait_ge(g_ag, 2)
                act.activation(sq[:], sq[:], ACT.Sqrt, bias=eps_t[:, 0:1]).then_inc(g_sq, 1)
                act.wait_ge(g_bn, 2)
                with act.Fori(0, NCH // NR) as j:
                    def relu1(u):
                        act.wait_ge(e_lh[u % 2], 16 * (NR // 2 * j + u // 2 + 1))
                        for t in range(CT):
                            v = h1w[:, u % 2, t * PX:(t + 1) * PX]
                            act.activation(v, v, ACT.Relu, bias=bias_b[:, 0, t:t + 1], scale=scale_b[:, 0, t:t + 1]).then_inc(e_r1, 1)

                    def relu2(u):
                        act.wait_ge(e_mac, NR * j + u + 1 + CR)
                        for t in range(CT):
                            v = h2[:, t, ds((NR * j + u) * PX, PX)]
                            i = act.activation(v, v, ACT.Relu, bias=bias_b[:, 1, t:t + 1], scale=1.0)
                        i.then_inc(e_r2, 1)
                    relu1(0)
                    for u in range(1, NR):
                        relu1(u)
                        relu2(u - 1)
                    relu2(NR - 1)

            @block2.vector
            def _(dve):
                def batch_norm(m, stats):
                    for t in range(CT):
                        i = dve.bn_aggr(mv2[:, t, :], stats[:, t].rearrange("p n s -> p (n s)"))
                    i.then_inc(g_bch, 1)
                    dve.wait_ge(g_bch, 4 * m + 1)
                    dve.tensor_copy(sq[:], mv2[:, :, 1]).then_inc(g_ag, 1)
                    dve.wait_ge(g_sq, m + 1)
                    dve.reciprocal(sq[:], sq[:]).then_inc(g_bch, 1)
                    dve.wait_ge(g_bch, 4 * m + 2)
                    dve.tensor_tensor(scale_b[:, m, :], sq[:], gb[:, 2 * m, :], ALU.mult).then_inc(g_bch, 1)
                    dve.wait_ge(g_bch, 4 * m + 3)
                    dve.tensor_tensor(bias_b[:, m, :], mv2[:, :, 0], scale_b[:, m, :], ALU.mult).then_inc(g_bch, 1)
                    dve.wait_ge(g_bch, 4 * m + 4)
                    dve.tensor_tensor(bias_b[:, m, :], gb[:, 2 * m + 1, :], bias_b[:, m, :], ALU.subtract).then_inc(g_bn, 1)

                batch_norm(0, bn1_stats)

                def planes(c):
                    dve.wait_ge(g_y, c.n + 1)
                    dve.wait_ge(g_split, c.n + CR)
                    if c.first or c.last:
                        edge = 0 if c.first else 9
                        dve.memset(xg[:, c.p, :, edge, :], 0.0).then_inc(g_edge, 1)
                        dve.wait_ge(g_edge, 2 * c.b + (1 if c.first else 2))
                    for j, (a, b, op) in enumerate(((0, 2, ALU.subtract), (1, 2, ALU.add), (2, 1, ALU.subtract), (1, 3, ALU.subtract))):
                        i = dve.tensor_tensor(V[:, :, j], xg[:, c.p, :, a:a + 2 * RP - 1:2, :], xg[:, c.p, :, b:b + 2 * RP - 1:2, :], op)
                    i.then_inc(g_v, 1)

                def rows_out(c):
                    dve.wait_ge(g_conv, c.n + 1 + CR)
                    dst = h2[:, :, ds(c.n * PX, PX)].rearrange("p t (i y w) -> p t i y w", y=2, w=W)
                    even, odd = dst[:, :, :, 0, :], dst[:, :, :, 1, :]
                    m = [psG[:, c.p, :, j, :].rearrange("p t (i w) -> p t i w", w=W) for j in range(PLANES)]
                    dve.tensor_copy(even, m[1]).then_inc(g_part, 1)
                    dve.wait_ge(g_part, 2 * c.n + 1)
                    dve.tensor_tensor(odd, even, m[2], ALU.subtract)
                    dve.tensor_tensor(even, even, m[0], ALU.add).then_inc(g_part, 1)
                    dve.wait_ge(g_part, 2 * c.n + 2)
                    dve.tensor_tensor(even, even, m[2], ALU.add)
                    dve.tensor_tensor(odd, odd, m[3], ALU.subtract).then_inc(g_h, 1)
                    dve.wait_ge(g_h, c.n + 1 + CR)
                    for t in range(CT):
                        i = dve.bn_stats(bn2_stats[:, t, ds(c.n, 1), :].rearrange("p r s -> p (r s)"), h2[:, t, ds(c.n * PX, PX)])
                    i.then_inc(g_stat, 1)

                AHEAD = 3

                def chunk(b, r):
                    return Chunk(b, r, r // 2, r % 2, r == 0, r == NR - 1)

                def batch(b, more):
                    for r in range(NR):
                        rows_out(chunk(b, r))
                        if r + AHEAD < NR:
                            planes(chunk(b, r + AHEAD))
                        elif more:
                            planes(chunk(b + 1, r + AHEAD - NR))
                for ready in (g_v, g_h, e_mac, e_sum):
                    dve.sem_inc(ready, CR)
                for r in range(AHEAD):
                    planes(chunk(0, r))
                with dve.Fori(0, NB - 1) as b:
                    batch(b, True)
                batch(NB - 1, False)
                dve.wait_ge(g_stat, NCH)
                batch_norm(1, bn2_stats)
                with dve.Fori(0, NCH // NR) as j:
                    def mix(u):
                        for t in range(CT):
                            dve.wait_ge(e_r1, CT * (NR * j + u) + t + 1)
                            v = h2[:, t, ds((NR * j + u) * PX, PX)]
                            i = dve.scalar_tensor_tensor(v, v, scale_b[:, 1, t:t + 1], h1w[:, u % 2, t * PX:(t + 1) * PX], ALU.mult, ALU.add)
                        i.then_inc(e_mac, 1)

                    def add_x1(u):
                        dve.wait_ge(e_r2, NR * j + u + 1)
                        dve.wait_ge(e_lx[u % 2], 16 * (NR // 2 * j + u // 2 + 1))
                        v = h2[:, :, ds((NR * j + u) * PX, PX)]
                        dve.tensor_tensor(v, v, x1w[:, u % 2, :].rearrange("p (t x) -> p t x", t=CT), ALU.add).then_inc(e_sum, 1)
                    mix(0)
                    for u in range(1, NR):
                        mix(u)
                        add_x1(u - 1)
                    add_x1(NR - 1)

            @block2.tensor
            def _(pe):
                def emit(c):
                    pe.wait_ge(g_split, c.n + 1 + CR)
                    pe.wait_ge(g_h, c.n - 1 + CR)
                    for j in range(PLANES):
                        for oc in range(CT):
                            for dx in range(3):
                                for t in range(CT):
                                    w = wino2[:, t, dx] if j == 2 else qw[:, t, (0, 3, None, 6)[j] + dx]
                                    for part in range(2):
                                        i = pe.matmul(psG[:, c.p, oc, j, :].rearrange("p (h w) -> p h w", h=RP), w[:, oc * 128:(oc + 1) * 128],
                                                      pg(c.p, part, t)[:, RP * j:RP * (j + 1), dx:dx + W],
                                                      start=(dx == 0 and t == 0 and part == 0),
                                                      stop=(dx == 2 and t == CT - 1 and part == 1))
                    i.then_inc(g_conv, 1)
                pe.sem_inc(g_conv, CR)
                batches(pe, emit)


def kernel(x, L0_conv_w_off, L0_conv_b_off, L0_conv_w_conv, L1_conv_w1, L1_conv_gamma1, L1_conv_beta1,
           L1_conv_w2, L1_conv_gamma2, L1_conv_beta2):
    import numpy as np
    import concourse.bacc as bacc
    from concourse import mybir
    from concourse.bass_utils import run_bass_kernel_spmd as run

    def by_input(w):
        w = np.asarray(w)
        return np.ascontiguousarray(w.reshape(w.shape[0], w.shape[1], 9).transpose(1, 2, 0))

    eye = np.eye(128, dtype=np.float32)
    group = np.kron(np.eye(16, dtype=np.float32), np.full((8, 8), 1 / 8, np.float32))
    sel = np.zeros((64, 27), np.float32)
    sel[np.arange(27), np.arange(27)] = 1
    sel[32 + np.arange(27), np.arange(27)] = 1
    p, r, t, k = np.ix_(np.arange(128), np.arange(8), np.arange(4), np.arange(9))
    grid = np.stack([8 * r + 2 * t + p // 64 + k // 3, p % 64 + k % 3 + 0 * (r + t)], axis=-1)
    grid = np.ascontiguousarray(grid.reshape(128, 8, 72).astype(np.float32))

    params = np.stack([np.asarray(v) for v in (L1_conv_gamma1, L1_conv_beta1, L1_conv_gamma2, L1_conv_beta2)])
    params = np.ascontiguousarray(params.reshape(4, 2, 128).transpose(2, 0, 1))

    ins = {"x": np.asarray(x), "w_off": by_input(L0_conv_w_off), "b_off": np.asarray(L0_conv_b_off),
           "w_conv": by_input(L0_conv_w_conv), "w1": by_input(L1_conv_w1), "w2": by_input(L1_conv_w2),
           "bn_params": params, "ident": eye, "group_avg": group, "sel_hl": sel, "base": grid}
    nc = bacc.Bacc("TRN2", target_bir_lowering=False, num_devices=1)
    args = [nc.dram_tensor(f"in_{n}", a.shape, mybir.dt.from_np(a.dtype), kind="ExternalInput").ap() for n, a in ins.items()]
    args.append(nc.dram_tensor("out", (4, 256, 64, 64), mybir.dt.float32, kind="ExternalOutput").ap())
    build(nc, *args)
    r = run(nc, [{f"in_{n}": a for n, a in ins.items()}], core_ids=[0])
    return r.results[0]["out"]
```
